# Optimizing a Trainium2 kernel written in Bass

```python
import numpy as np
import jax
import jax.numpy as jnp

def _softmax(x, axis=-1):
    return jax.nn.softmax(x, axis=axis)

def _gelu(x):
    return jax.nn.gelu(x, approximate=True)

def _silu(x):
    return jax.nn.silu(x)

def _sigmoid(x):
    return jax.nn.sigmoid(x)

def _layernorm(x, axis=-1, eps=1e-05):
    m = jnp.mean(x, axis=axis, keepdims=True)
    v = jnp.var(x, axis=axis, keepdims=True)
    return (x - m) / jnp.sqrt(v + eps)

def _scatter_add(tgt, idx, src, axis=0):
    return tgt.at[idx].add(src)

def _segment_sum(src, seg, n):
    return jax.ops.segment_sum(src, seg, n)
kernel_name = 'mk_gnn_preln_d2_gnn_r8_21c2f5'

def setup_inputs(seed: int=0):
    np.random.seed(seed)
    _w = jnp.asarray

    def _rec_inputs():
        import jax
        import jax.numpy as jnp
        _gk = jax.random.key(seed)
        x = -0.0005121 + 1.001 * jax.random.normal(jax.random.fold_in(_gk, 1), (12500, 32), jnp.float32)
        _s = jax.random.randint(jax.random.fold_in(_gk, 2), (200000,), 0, 12500, jnp.int32)
        _d = jax.random.randint(jax.random.fold_in(_gk, 3), (200000,), 0, 12500, jnp.int32)
        _loop = jnp.arange(12500, dtype=jnp.int32)
        src = jnp.concatenate([_s, _d, _loop])
        dst = jnp.concatenate([_d, _s, _loop])
        _o = jnp.argsort(dst, stable=True)
        src = src[_o]
        dst = dst[_o]
        edge_attr_4 = 0.00086875 + 0.999764 * jax.random.normal(jax.random.fold_in(_gk, 11), (412500, 4), jnp.float32)
        edge_attr_8 = jax.random.uniform(jax.random.fold_in(_gk, 12), (412500, 8), jnp.float32, 0.0, 1)
        edge_weight = jax.random.uniform(jax.random.fold_in(_gk, 14), (412500,), jnp.float32, 0.0, 1)
        return (x, src, dst, edge_attr_4, edge_attr_8, edge_weight)
    x, src, dst, edge_attr_4, edge_attr_8, edge_weight = _rec_inputs()

    def _L0_gnn_setup():
        import jax, jax.numpy as jnp
        import numpy as np
        N_NODES = 12500
        N_EDGES = 200000
        N_FEAT = 32
        key = jax.random.key(seed)
        k1, k2, k3, k4 = jax.random.split(key, 4)
        u = jax.random.normal(k1, (N_NODES, N_FEAT), dtype=jnp.float32)
        weights = jax.random.uniform(k2, (N_EDGES,), dtype=jnp.float32)
        row = jax.random.randint(k3, (N_EDGES,), 0, N_NODES)
        col = jax.random.randint(k4, (N_EDGES,), 0, N_NODES)
        edge_index = jnp.stack([row, col]).astype(jnp.int64)
        return {'u': u, 'weights': weights, 'edge_index': edge_index}
    _L0_gnn_all = _L0_gnn_setup()
    _L0_gnn_in = {k: v for k, v in _L0_gnn_all.items() if k in ()}
    del _L0_gnn_all

    def _L1_gnn_setup():
        import jax, jax.numpy as jnp
        import numpy as np
        N = 4096
        E = 65536
        MUL = 8
        NB = 8
        HR = 64
        NTP = 4 * MUL * MUL
        AVG_NEI = 16.0
        INV_SQRT3 = 1.0 / np.sqrt(3.0)
        ALPHA = 1.0 / np.sqrt(2.0 * MUL)
        key = jax.random.key(seed)
        ks = jax.random.split(key, 12)
        h = jax.random.normal(ks[0], (N, 4 * MUL), jnp.float32)
        edge_index = jax.random.randint(ks[1], (2, E), 0, N)
        edge_sh = jax.random.normal(ks[2], (E, 4), jnp.float32)
        edge_radial = jax.random.uniform(ks[3], (E, NB), jnp.float32)

        def lin(k, fi, fo):
            return (jax.random.normal(k, (fi, fo), jnp.float32) / np.sqrt(fi)).astype(jnp.float32)
        W1 = lin(ks[4], NB, HR)
        b1 = jnp.zeros((HR,), jnp.float32)
        W2 = lin(ks[5], HR, HR)
        b2 = jnp.zeros((HR,), jnp.float32)
        W3 = lin(ks[6], HR, NTP)
        b3 = jnp.zeros((NTP,), jnp.float32)
        Ws = jax.random.normal(ks[7], (MUL, MUL), jnp.float32)
        Wv = jax.random.normal(ks[8], (MUL, MUL), jnp.float32)
        return dict(h=h, edge_index=edge_index, edge_sh=edge_sh, edge_radial=edge_radial, n_atoms=N, W1=W1, b1=b1, W2=W2, b2=b2, W3=W3, b3=b3, Ws=Ws, Wv=Wv)
    _L1_gnn_all = _L1_gnn_setup()
    _L1_gnn_in = {k: v for k, v in _L1_gnn_all.items() if k in ('W1', 'b1', 'W2', 'b2', 'W3', 'b3', 'Ws', 'Wv')}
    del _L1_gnn_all
    return {'x': x, 'src': src, 'dst': dst, 'edge_attr_4': edge_attr_4, 'edge_attr_8': edge_attr_8, 'edge_weight': edge_weight, 'L1_gnn_W1': _L1_gnn_in['W1'], 'L1_gnn_b1': _L1_gnn_in['b1'], 'L1_gnn_W2': _L1_gnn_in['W2'], 'L1_gnn_b2': _L1_gnn_in['b2'], 'L1_gnn_W3': _L1_gnn_in['W3'], 'L1_gnn_b3': _L1_gnn_in['b3'], 'L1_gnn_Ws': _L1_gnn_in['Ws'], 'L1_gnn_Wv': _L1_gnn_in['Wv']}

def reference(x, src, dst, edge_attr_4, edge_attr_8, edge_weight, L1_gnn_W1, L1_gnn_b1, L1_gnn_W2, L1_gnn_b2, L1_gnn_W3, L1_gnn_b3, L1_gnn_Ws, L1_gnn_Wv):
    import jax
    import jax.numpy as jnp

    def _L0_gnn_ref(u, weights, edge_index):
        import jax, jax.numpy as jnp
        import numpy as np
        N_NODES = 12500
        N_EDGES = 200000
        N_FEAT = 32
        row, col = (edge_index[0], edge_index[1])
        diff = u[col] - u[row]
        weighted_diff = weights[:, None] * diff
        laplacian = jax.ops.segment_sum(weighted_diff, row, num_segments=u.shape[0])
        return laplacian

    def _L1_gnn_ref(h, edge_index, edge_sh, edge_radial, n_atoms, W1, b1, W2, b2, W3, b3, Ws, Wv):
        import jax, jax.numpy as jnp
        import numpy as np
        N = 4096
        E = 65536
        MUL = 8
        NB = 8
        HR = 64
        NTP = 4 * MUL * MUL
        AVG_NEI = 16.0
        INV_SQRT3 = 1.0 / np.sqrt(3.0)
        ALPHA = 1.0 / np.sqrt(2.0 * MUL)
        src, dst = (edge_index[0], edge_index[1])
        x = jax.nn.silu(edge_radial @ W1 + b1)
        x = jax.nn.silu(x @ W2 + b2)
        tpw = x @ W3 + b3
        P = MUL * MUL
        W00 = tpw[:, 0 * P:1 * P].reshape(-1, MUL, MUL)
        W110 = tpw[:, 1 * P:2 * P].reshape(-1, MUL, MUL)
        W01 = tpw[:, 2 * P:3 * P].reshape(-1, MUL, MUL)
        W10 = tpw[:, 3 * P:4 * P].reshape(-1, MUL, MUL)
        hs = h[:, :MUL]
        hv = h[:, MUL:].reshape(-1, MUL, 3)
        hs_e = hs[src]
        hv_e = hv[src]
        sh0 = edge_sh[:, 0]
        sh1 = edge_sh[:, 1:4]
        m0 = ALPHA * (jnp.einsum('eu,euw->ew', hs_e * sh0[:, None], W00) + INV_SQRT3 * jnp.einsum('eui,ei,euw->ew', hv_e, sh1, W110))
        m1 = ALPHA * (jnp.einsum('eu,ei,euw->ewi', hs_e, sh1, W01) + jnp.einsum('eui,euw->ewi', hv_e * sh0[:, None, None], W10))
        messages = jnp.concatenate([m0, m1.reshape(-1, 3 * MUL)], axis=-1)
        agg = jax.ops.segment_sum(messages, dst, num_segments=n_atoms) / np.sqrt(AVG_NEI)
        self0 = hs @ Ws / np.sqrt(MUL)
        self1 = jnp.einsum('nui,uw->nwi', hv, Wv) / np.sqrt(MUL)
        h_self = jnp.concatenate([self0, self1.reshape(-1, 3 * MUL)], axis=-1)
        return h_self + agg
    edge_index = jnp.stack([src, dst])
    h = jnp.maximum(_layernorm(x, axis=-1), 0.0)
    x = x + _L0_gnn_ref(h, edge_weight, edge_index)
    h = jnp.maximum(_layernorm(x, axis=-1), 0.0)
    x = x + _L1_gnn_ref(h, edge_index, edge_attr_4, edge_attr_8, 12500, L1_gnn_W1, L1_gnn_b1, L1_gnn_W2, L1_gnn_b2, L1_gnn_W3, L1_gnn_b3, L1_gnn_Ws, L1_gnn_Wv)
    return x

_drawn_inputs = setup_inputs


def setup_inputs(seed=0):
    import zlib

    import numpy as np

    out = dict(_drawn_inputs(seed))
    spreads = {'L1_gnn_b1': (0.0, 0.8), 'L1_gnn_b2': (0.0, 2.0), 'L1_gnn_b3': (0.0, 2.0)}
    factors = {'edge_attr_4': 3.277,
     'edge_attr_8': 8.0,
     'L1_gnn_W1': 4.36,
     'L1_gnn_W2': 4.191,
     'L1_gnn_W3': 3.986,
     'L1_gnn_Ws': 64.0,
     'L1_gnn_Wv': 51.023}
    for name, (base, spread) in spreads.items():
        noise = np.random.default_rng([zlib.crc32(name.encode()), seed]).standard_normal(out[name].shape)
        drawn = base * np.exp(spread * noise) if base else spread * noise
        out[name] = jnp.asarray(drawn.astype(out[name].dtype))
    for name, factor in factors.items():
        out[name] = (out[name] * factor).astype(out[name].dtype)
    return out
```

```python
import concourse.bass as bass
from concourse import mybir
from contextlib import ExitStack
from math import sqrt

P = 128
F = 32
MUL = 8
FW = F + 1
PARTS = 3
TILES = 16
GE = TILES * P
HALF = GE // 2
CT = 4
CH = TILES // CT
BC = 2 * CH
NTAB = 8
HR = 64
WN = 4 * MUL * MUL
SUMS = 5
RS = 2 * MUL * MUL
RC = RS + 3 * SUMS * MUL
NP = 125
EPS = 1e-5
AVG_NEI = 16.0
MSG_SCALE = 1.0 / sqrt(2.0 * MUL) / sqrt(AVG_NEI)
SELF_SCALE = 1.0 / sqrt(MUL)


def rounds_of(n_nodes):
    return -(-(n_nodes + 1) // P)


def table_rows(n_nodes):
    return max(-(-(n_nodes + 1 + P) // P), rounds_of(n_nodes) + 1) * P


def gnn_program(nc, x, src_row, dst_row, src_col, dst_col, w_col, sh_col, radial,
                W1, b1, W2, b2, W3, b3, Ws, Wv, out):
    f32, bf16, i32 = mybir.dt.float32, mybir.dt.bfloat16, mybir.dt.int32
    ALU, ACT, AX = mybir.AluOpType, mybir.ActivationFunctionType, mybir.AxisListType.X
    N = x.shape[0]
    G = radial.shape[0]
    G2 = G // 2
    RM, NT = rounds_of(N), table_rows(N)
    C = N // NP
    CE = G * GE // P
    TAIL = NT - N
    BW = G + 2

    def table(name, shape, dt=f32):
        return nc.dram_tensor(name, shape, dt, kind="Internal").ap()

    h1_tab = table("h1_tab", (NT, PARTS * FW), bf16)
    h2_tab = table("h2_tab", (NT, F))
    agg_tab = table("agg_tab", (NT, F))
    lap_tab = [table(f"lap_tab{k}", (NT, FW)) for k in range(NTAB)]
    digits = table("digits", (2, 2, G * GE), bf16)
    hidden = table("hidden", (G + 1, P, HALF))
    base_f = table("base_f", (1, RM * BW))
    base_i = table("base_i", (1, RM * BW), i32)

    whole = ExitStack()
    with whole:
        def sb(ctx, name, shape, dt=f32):
            return ctx.enter_context(nc.sbuf_tensor(name, shape, dt))

        def pb(ctx, name, shape, dt=f32):
            return ctx.enter_context(nc.psum_tensor(name, shape, dt))

        def sem(name):
            return whole.enter_context(nc.semaphore(name))

        iota_row = sb(whole, "iota_row", [P, P])
        iota_col = sb(whole, "iota_col", [P, 1])
        spare_col = sb(whole, "spare_col", [P, 1])
        ident = sb(whole, "ident", [P, P])
        upper = sb(whole, "upper", [P, P])
        x_sb = sb(whole, "x_sb", [NP, C, F])
        h1_sb = sb(whole, "h1_sb", [NP, C, FW])
        w1_bd = sb(whole, "w1_bd", [2 * MUL, P])
        w2_bd = sb(whole, "w2_bd", [P, P])
        b1_col = sb(whole, "b1_col", [P, 1])
        b2_col = sb(whole, "b2_col", [P, 1])
        w3_sb = sb(whole, "w3_sb", [HR + 1, WN])
        self_bd = sb(whole, "self_bd", [P, P])
        place_val = sb(whole, "place_val", [2, P], bf16)
        rounds = sb(whole, "rounds", [1, 1], i32)
        eps_col = sb(whole, "eps_col", [P, 1])

        dve_step = sem("dve_step")
        passed = sem("passed")
        steps = {"dve": 0}

        def then(dve, ins):
            steps["dve"] += 1
            ins.then_inc(dve_step, 1)
            dve.wait_ge(dve_step, steps["dve"])

        def center(dve, rows, mean, xc, centered):
            then(dve, nc.vector.tensor_reduce(mean[:], rows, axis=AX, op=ALU.add))
            then(dve, nc.vector.tensor_scalar(mean[:], mean[:], 1.0 / F, None, ALU.mult))
            nc.vector.tensor_tensor(xc[:], rows, mean[:].unsqueeze(2).to_broadcast([NP, C, F]),
                                    ALU.subtract).then_inc(centered, 1)

        def normalise(dve, sq, mean, std, xc, normed, squared, var_ready, std_ready, h_ready):
            dve.wait_ge(squared, 1)
            nc.vector.tensor_reduce(mean[:], sq, axis=AX, op=ALU.add).then_inc(var_ready, 1)
            dve.wait_ge(std_ready, 1)
            then(dve, nc.vector.reciprocal(std[:], std[:]))
            nc.vector.scalar_tensor_tensor(normed, xc[:], 0.0, std[:].unsqueeze(2).to_broadcast([NP, C, F]),
                                           ALU.max, ALU.mult).then_inc(h_ready, 1)

        x_in, idx_in, rows_in, w_in = sem("x_in"), sem("idx_in"), sem("rows_in"), sem("w_in")
        iota_done, cleared, zero_ready = sem("iota_done"), sem("cleared"), sem("zero_ready")
        first_ready, first_seen, bad_ready, bad_seen = sem("first_ready"), sem("first_seen"), sem("bad_ready"), sem("bad_seen")
        split = [sem("split_dst"), sem("split_src")]
        centered, squared, var_ready, std_ready, h1_ready, rest_ready = (
            sem("centered"), sem("squared"), sem("var_ready"), sem("std_ready"), sem("h1_ready"), sem("rest_ready"))
        part_ready, digits_seen = sem("part_ready"), sem("digits_seen")
        added = [sem(f"added{k}") for k in range(NTAB)]
        base_ready, sp_out, act_out = sem("base_ready"), sem("sp_out"), sem("act_out")

        prep = ExitStack()
        with prep:
            iota_i = sb(prep, "iota_i", [P, P + 1], i32)
            ones = sb(prep, "ones", [P, P])
            zeros = sb(prep, "zeros", [P, max(NT // P, TAIL // 4) * FW])
            zeros_b = sb(prep, "zeros_b", [4, TAIL // 4 * PARTS * FW], bf16)
            row_i = [sb(prep, f"row_i{a}", [P, CE], i32) for a in range(2)]
            high_i = [sb(prep, f"high_i{a}", [P, CE], i32) for a in range(2)]
            digit_b = sb(prep, "digit_b", [P, 2, 2, CE], bf16)
            first_i = sb(prep, "first_i", [1, G], i32)
            first_f = sb(prep, "first_f", [1, G])
            dst_i = sb(prep, "dst_i", [P, G, TILES], i32)
            off = sb(prep, "off", [P, G, TILES])
            ext = sb(prep, "ext", [P, 2])
            bad = sb(prep, "bad", [P, 1])
            sel = sb(prep, "sel", [P, 5])
            base_sb = sb(prep, "base_sb", [P, BW])
            base_isb = sb(prep, "base_isb", [P, BW], i32)
            mean = sb(prep, "mean", [NP, C])
            std = sb(prep, "std", [NP, C])
            rest = sb(prep, "rest", [NP, C, FW])
            sq = rest[:, :, 0:F]
            xc = sb(prep, "xc", [NP, C, F])
            w3_raw = sb(prep, "w3_raw", [HR + 1, WN])
            first_ps = pb(prep, "first_ps", [P, 512])
            bad_ps = pb(prep, "bad_ps", [P, 512])
            h1_b = sb(prep, "h1_b", [NP, C, PARTS, FW], bf16)
            W_LOADS = 4 * 2 + 2 + 4 * 4

            block = prep.enter_context(nc.Block("prepare"))

            @block.sync
            def _(sp):
                sp.dma_start(x_sb[:].rearrange("p c f -> p (c f)"),
                             x.rearrange("(p c) f -> p (c f)", p=NP)).then_inc(x_in, 16)
                sp.dma_start(dst_i[:].rearrange("p g t -> p (g t)"), dst_col[:, 0:G * TILES]).then_inc(idx_in, 16)
                sp.dma_start(first_i[:], dst_row.rearrange("(a g e) -> a g e", a=1, e=GE)[:, :, 0],
                             allow_slow_non_contiguous=True).then_inc(idx_in, 16)
                for a, row in enumerate((dst_row, src_row)):
                    sp.dma_start(row_i[a][:], row.rearrange("(p c) -> p c", p=P)).then_inc(rows_in, 16)
                for a in range(2):
                    sp.wait_ge(split[a], 2)
                    for d in range(2):
                        sp.dma_start(digits[d, a].rearrange("(p c) -> p c", p=P), digit_b[:, d, a, :]).then_inc(sp_out, 16)
                sp.wait_ge(part_ready, PARTS)
                sp.dma_start(h1_tab[0:N, :].rearrange("(p c) f -> p (c f)", p=NP),
                             h1_b[:].rearrange("p c k f -> p (c k f)")).then_inc(sp_out, 16)
                sp.wait_ge(base_ready, 2)
                sp.dma_start(base_f.rearrange("a (r g) -> (a r) g", g=BW), base_sb[0:RM, :]).then_inc(sp_out, 16)
                sp.dma_start(base_i.rearrange("a (r g) -> (a r) g", g=BW), base_isb[0:RM, :]).then_inc(sp_out, 16)
                sp.wait_ge(sp_out, 16 * 7)

            @block.gpsimd
            def _(pool):
                nc.gpsimd.iota(iota_i[:, 0:P], pattern=[[1, P]], base=0, channel_multiplier=0).then_inc(iota_done, 1)
                nc.gpsimd.iota(iota_i[:, P:P + 1], pattern=[[1, 1]], base=0, channel_multiplier=1).then_inc(iota_done, 1)
                for tile in (w1_bd, w2_bd, self_bd):
                    nc.gpsimd.memset(tile[:], 0.0).then_inc(cleared, 1)
                nc.gpsimd.memset(ones[:], 1.0).then_inc(cleared, 1)
                nc.gpsimd.memset(eps_col[:], EPS).then_inc(cleared, 1)
                nc.gpsimd.memset(zeros_b[:], 0.0)
                nc.gpsimd.memset(zeros[:], 0.0).then_inc(zero_ready, 1)
                pool.wait_ge(zero_ready, 1)
                for k in range(NTAB):
                    pool.dma_start(lap_tab[k].rearrange("(p c) f -> p (c f)", p=P),
                                   zeros[:, 0:NT // P * FW]).then_inc(added[k], 16)
                for k in range(NTAB):
                    pool.wait_ge(added[k], 16)

            @block.scalar
            def _(act):
                act.wait_ge(cleared, 5)
                for k in range(2):
                    act.dma_start(w1_bd[MUL * k:MUL * k + MUL, HR * k:HR * k + HR], W1).then_inc(w_in, 16)
                    act.dma_start(w2_bd[HR * k:HR * k + HR, HR * k:HR * k + HR], W2).then_inc(w_in, 16)
                    act.dma_start(b1_col[HR * k:HR * k + HR, :], b1.rearrange("(p a) -> p a", a=1)).then_inc(w_in, 16)
                    act.dma_start(b2_col[HR * k:HR * k + HR, :], b2.rearrange("(p a) -> p a", a=1)).then_inc(w_in, 16)
                act.dma_start(w3_raw[0:HR, :], W3).then_inc(w_in, 16)
                act.dma_start(w3_raw[HR:HR + 1, :], b3.rearrange("(a n) -> a n", a=1)).then_inc(w_in, 16)
                for k in range(4):
                    o = F * k
                    act.dma_start(self_bd[o:o + MUL, o:o + MUL], Ws).then_inc(w_in, 16)
                    for i in range(3):
                        v = o + MUL + i
                        act.dma_start(self_bd[v:o + F:3, v:o + F:3], Wv, allow_slow_non_contiguous=True).then_inc(w_in, 16)
                act.wait_ge(centered, 1)
                nc.scalar.activation(sq, xc[:], ACT.Square).then_inc(squared, 1)
                act.wait_ge(var_ready, 1)
                nc.scalar.activation(std[:], mean[:], ACT.Sqrt, scale=1.0 / F, bias=eps_col[0:NP, :]).then_inc(std_ready, 1)
                act.wait_ge(h1_ready, 1)
                nc.scalar.activation(h1_b[:, :, 0, :], h1_sb[:], ACT.Copy).then_inc(part_ready, 1)
                act.wait_ge(rest_ready, 1)
                nc.scalar.activation(h1_b[:, :, 1, :], rest[:], ACT.Copy).then_inc(part_ready, 1)
                for a in range(2):
                    for d in range(2):
                        act.wait_ge(digits_seen, 2 * a + d + 1)
                        nc.scalar.activation(digit_b[:, d, a, :], (high_i, row_i)[d][a][:], ACT.Copy).then_inc(split[a], 1)
                act.wait_ge(zero_ready, 1)
                act.dma_start(h1_tab[N:NT, :].rearrange("(p c) f -> p (c f)", p=4),
                              zeros_b[:]).then_inc(act_out, 16)
                for tab in (h2_tab, agg_tab):
                    act.dma_start(tab[N:NT, :].rearrange("(p c) f -> p (c f)", p=4),
                                  zeros[0:4, 0:TAIL // 4 * F]).then_inc(act_out, 16)
                act.wait_ge(act_out, 16 * 3)

            @block.tensor
            def _(pe):
                pe.wait_ge(cleared, 5)
                pe.wait_ge(first_ready, 1)
                nc.tensor.matmul(first_ps[:, 0:G], ones[0:1, :], first_f[:], start=True, stop=True).then_inc(first_seen, 1)
                pe.wait_ge(bad_ready, 1)
                nc.tensor.matmul(bad_ps[:, 0:1], ones[:], bad[:], start=True, stop=True).then_inc(bad_seen, 1)

            @block.vector
            def _(dve):
                dve.wait_ge(iota_done, 2)
                nc.vector.tensor_copy(iota_row[:], iota_i[:, 0:P])
                then(dve, nc.vector.tensor_copy(iota_col[:], iota_i[:, P:P + 1]))
                nc.vector.tensor_scalar(upper[:], iota_row[:], iota_col[:], None, ALU.is_ge)
                nc.vector.tensor_scalar(ident[:], iota_row[:], iota_col[:], None, ALU.is_equal)
                nc.vector.tensor_scalar(spare_col[:], iota_col[:], float(N + 1), None, ALU.add)
                then(dve, nc.vector.tensor_scalar(sel[:, 0:1], iota_col[:], float(1 - P), float(P), ALU.mult, ALU.add))
                nc.vector.tensor_scalar(place_val[:], iota_row[0:2, :], 0.0, sel[0:2, 0:1], ALU.mult, ALU.add)
                nc.vector.memset(h1_sb[:, :, F:FW], 1.0)
                dve.wait_ge(x_in, 16)
                center(dve, x_sb[:], mean, xc, centered)
                dve.wait_ge(idx_in, 32)
                nc.vector.tensor_copy(first_f[:], first_i[:]).then_inc(first_ready, 1)
                normalise(dve, sq, mean, std, xc, h1_sb[:, :, 0:F], squared, var_ready, std_ready, h1_ready)
                dve.wait_ge(part_ready, 1)
                nc.vector.tensor_tensor(rest[:], h1_sb[:], h1_b[:, :, 0, :], ALU.subtract).then_inc(rest_ready, 1)
                dve.wait_ge(w_in, 16 * W_LOADS)
                m2 = MUL * MUL
                nc.vector.tensor_scalar(w3_sb[:, 0:m2], w3_raw[:, m2:2 * m2], 1.0 / sqrt(3.0), None, ALU.mult)
                nc.vector.tensor_copy(w3_sb[:, m2:2 * m2], w3_raw[:, 0:m2])
                nc.vector.tensor_copy(w3_sb[:, 2 * m2:WN], w3_raw[:, 2 * m2:WN])
                dve.wait_ge(rows_in, 32)
                for a in range(2):
                    nc.vector.tensor_single_scalar(high_i[a][:], row_i[a][:], 7, op=ALU.logical_shift_right).then_inc(digits_seen, 1)
                    dve.wait_ge(digits_seen, 2 * a + 1)
                    nc.vector.tensor_single_scalar(row_i[a][:], row_i[a][:], P - 1, op=ALU.bitwise_and).then_inc(digits_seen, 1)
                dve.wait_ge(part_ready, 2)
                nc.vector.tensor_tensor(h1_b[:, :, 2, :], rest[:], h1_b[:, :, 1, :], ALU.subtract).then_inc(part_ready, 1)
                dve.wait_ge(first_seen, 1)
                then(dve, nc.vector.tensor_tensor(off[:], dst_i[:], first_ps[:, 0:G].unsqueeze(2).to_broadcast([P, G, TILES]),
                                                  ALU.subtract))
                nc.vector.tensor_reduce(ext[:, 0:1], off[:].rearrange("p g t -> p (g t)"), axis=AX, op=ALU.max)
                then(dve, nc.vector.tensor_reduce(ext[:, 1:2], off[:].rearrange("p g t -> p (g t)"), axis=AX, op=ALU.min))
                nc.vector.tensor_scalar(ext[:, 0:1], ext[:, 0:1], float(P - 1), None, ALU.is_gt)
                then(dve, nc.vector.tensor_scalar(ext[:, 1:2], ext[:, 1:2], 0.0, None, ALU.is_lt))
                nc.vector.tensor_tensor(bad[:], ext[:, 0:1], ext[:, 1:2], ALU.add).then_inc(bad_ready, 1)
                dve.wait_ge(bad_seen, 1)
                then(dve, nc.vector.tensor_scalar(sel[:, 0:1], bad_ps[:, 0:1], 1.0, None, ALU.min))
                nc.vector.tensor_scalar(sel[:, 1:2], sel[:, 0:1], -1.0, 1.0, ALU.mult, ALU.add)
                nc.vector.tensor_scalar(rounds[:], sel[0:1, 0:1], float(RM - 1), 1.0, ALU.mult, ALU.add)
                nc.vector.tensor_scalar(sel[:, 2:3], iota_col[:], float(P), None, ALU.mult)
                nc.vector.tensor_scalar(sel[:, 4:5], iota_col[:], float(P), float(P), ALU.mult, ALU.add)
                then(dve, nc.vector.tensor_scalar(sel[:, 3:4], iota_col[:], -1.0, 0.0, ALU.add, ALU.max))
                then(dve, nc.vector.tensor_scalar(sel[:, 3:4], sel[:, 3:4], float(P), None, ALU.mult))
                then(dve, nc.vector.tensor_scalar(sel[:, 2:5], sel[:, 2:5], sel[:, 0:1], None, ALU.mult))
                for cols, of, s in ((slice(1, G + 1), slice(0, G), 2), (slice(0, 1), slice(0, 1), 3),
                                    (slice(G + 1, BW), slice(0, 1), 4)):
                    last = nc.vector.tensor_scalar(base_sb[:, cols], first_ps[:, of], sel[:, 1:2], sel[:, s:s + 1],
                                                   ALU.mult, ALU.add)
                last.then_inc(base_ready, 1)
                dve.wait_ge(base_ready, 1)
                nc.vector.tensor_copy(base_isb[:], base_sb[:]).then_inc(base_ready, 1)

        L0_LOADS = 6
        AHEAD = CH + 1
        l0_in = [sem("l0_in0"), sem("l0_in1")]
        rows_ready, rows_read = sem("rows_ready"), sem("rows_read")
        mlp_ready, silu_done = sem("mlp_ready"), sem("silu_done")
        pick_ready, picked, msg_ready, merged = sem("pick_ready"), sem("picked"), sem("msg_ready"), sem("merged")
        sums_ready, where_ready = sem("sums_ready"), sem("where_ready")
        stored = [sem("stored0"), sem("stored1")]
        link0 = sem("link0")
        ADDS = 2 * TILES // NTAB
        landed = sem("landed")
        LANDED_AHEAD = 2 * TILES - CT - NTAB + 1

        lay0 = ExitStack()
        with lay0:
            digit_sb = sb(lay0, "digit_sb", [2, 2, 2, GE], bf16)
            rad_sb = sb(lay0, "rad_sb", [2 * MUL, 2, HALF])
            win_sb = sb(lay0, "win_sb", [P, 2, PARTS, FW], bf16)
            src_i = sb(lay0, "src_i", [P, 2, TILES], i32)
            w_sb = sb(lay0, "w_sb", [P, 2, TILES])
            base_in = sb(lay0, "base_in", [P, 2])
            node_col = sb(lay0, "node_col", [P, 1])
            src_f = sb(lay0, "src_f", [P, TILES])
            to_spare = sb(lay0, "to_spare", [P, TILES])
            pick = sb(lay0, "pick", [P, 2, CT, P], bf16)
            same = sb(lay0, "same", [P, 2, CT, P], bf16)
            later = sb(lay0, "later", [P, CT])
            hop = sb(lay0, "hop", [P, CT])
            where = sb(lay0, "where", [P, 2, TILES], i32)
            msg = sb(lay0, "msg", [P, CT, FW])
            left = sb(lay0, "left", [P, CT, FW])
            msg_b = sb(lay0, "msg_b", [P, 2, PARTS, CT, FW], bf16)
            sums = sb(lay0, "sums", [P, 2, TILES, FW])
            hid1 = sb(lay0, "hid1", [P, 2, 512])
            hid2 = sb(lay0, "hid2", [P, 2, HALF])
            rows_ps = pb(lay0, "rows_ps", [P, 2, 2, 512])
            mlp_ps = pb(lay0, "mlp_ps", [P, 2, 512])
            pick_ps = pb(lay0, "pick_ps", [P, 512])
            sums_ps = pb(lay0, "sums_ps", [P, 512])

            picks, totals = (tile[:, 0:CT * FW].rearrange("p (t f) -> p t f", f=FW) for tile in (pick_ps, sums_ps))

            block = lay0.enter_context(nc.Block("layer0"))

            @block.sync
            def _(sp):
                R = sp.value_load(rounds[0:1, 0:1], min_val=1, max_val=RM)
                with sp.Fori(0, R) as r, sp.Fori(0, G2) as g2:
                    i = r * G2 + g2
                    for s in range(2):
                        g = g2 * 2 + s
                        sp.wait_ge(msg_ready, (i * 2 + s - 1) * CH + AHEAD)
                        sp.wait_ge(merged, (i * 2 + s - 1) * CH + AHEAD)
                        sp.sem_inc(passed, 1)
                        sp.dma_start(digit_sb[:, s, :, :], digits[:, :, bass.ds(g * GE, GE)]).then_inc(l0_in[s], 16)
                        sp.dma_start(rad_sb[:, s, :], radial[bass.ds(g, 1), :, :].rearrange("a p c -> (a p) c")).then_inc(l0_in[s], 16)
                        sp.dma_start(src_i[:, s, :], src_col[:, bass.ds(g * TILES, TILES)]).then_inc(l0_in[s], 16)
                        sp.dma_start(w_sb[:, s, :], w_col[:, bass.ds(g * TILES, TILES)]).then_inc(l0_in[s], 16)
                        at = r * BW + g + 1
                        sp.dma_start(base_in[:, s:s + 1], base_f[:, bass.ds(at, 1)].to_broadcast([P, 1]),
                                     allow_slow_non_contiguous=True).then_inc(l0_in[s], 16)
                        base = sp.value_load(base_i[:, bass.ds(at, 1)], min_val=0, max_val=NT - P)
                        sp.dma_start(win_sb[:, s, :, :].rearrange("p k f -> p (k f)"), h1_tab[bass.ds(base, P), :]).then_inc(l0_in[s], 16)

            @block.tensor
            def _(pe):
                pe.sem_inc(merged, AHEAD)
                R = pe.value_load(rounds[0:1, 0:1], min_val=1, max_val=RM)

                def sum_same(i, c):
                    pe.wait_ge(msg_ready, i * BC + c + 1 + AHEAD)
                    pe.wait_ge(sums_ready, i * BC + c + 2)
                    for t in range(CT):
                        for k in range(PARTS):
                            last = nc.tensor.matmul(totals[:, t, :], same[:, c % 2, t, :], msg_b[:, c % 2, k, t, :],
                                                    start=(k == 0), stop=(k == PARTS - 1))
                    last.then_inc(merged, 1)

                with pe.Fori(0, R) as r, pe.Fori(0, G2) as g2:
                    i = r * G2 + g2
                    for c in range(BC):
                        s, q = divmod(c, CH)
                        if q == 0:
                            pe.wait_ge(l0_in[s], (i + 1) * (16 * L0_LOADS))
                        pe.wait_ge(rows_read, i * BC + c + 1)
                        for a in range(2):
                            last = nc.tensor.matmul(rows_ps[:, c % 2, a, :], place_val[:],
                                                    digit_sb[:, s, a, q * CT * P:(q + 1) * CT * P], start=True, stop=True)
                        last.then_inc(rows_ready, 1)
                        h = q % 2
                        pe.wait_ge(silu_done, i * BC + c + 1)
                        if q < 2:
                            last = nc.tensor.matmul(mlp_ps[:, h, :], w1_bd[:], rad_sb[:, s, h * 512:(h + 1) * 512],
                                                    start=True, stop=True)
                        else:
                            last = nc.tensor.matmul(mlp_ps[:, h, :], w2_bd[:], hid1[:, h, :], start=True, stop=True)
                        last.then_inc(mlp_ready, 1)
                        if c:
                            sum_same(i, c - 1)
                        pe.wait_ge(pick_ready, i * BC + c + 1)
                        for t in range(CT):
                            for k in range(PARTS):
                                last = nc.tensor.matmul(picks[:, t, :], pick[:, c % 2, t, :], win_sb[:, s, k, :],
                                                        start=(k == 0), stop=(k == PARTS - 1))
                        last.then_inc(picked, 1)
                    sum_same(i, BC - 1)

            @block.scalar
            def _(act):
                act.sem_inc(silu_done, 2)
                act.sem_inc(sums_ready, 2)
                for s in range(2):
                    act.dma_start(hidden[G, :, s:s + 1], b1_col[:], allow_slow_non_contiguous=True).then_inc(stored[s], 16)
                R = act.value_load(rounds[0:1, 0:1], min_val=1, max_val=RM)

                def copy_sums(i, c):
                    s, q = divmod(c, CH)
                    act.wait_ge(merged, i * BC + c + 1 + AHEAD)
                    act.wait_ge(landed, i * (2 * TILES) + c * CT + 1)
                    nc.scalar.activation(sums[:, s, q * CT:(q + 1) * CT, :], totals,
                                         ACT.Copy).then_inc(sums_ready, 1)

                with act.Fori(0, R) as r, act.Fori(0, G2) as g2:
                    i = r * G2 + g2
                    for c in range(BC):
                        s, q = divmod(c, CH)
                        h = q % 2
                        act.wait_ge(mlp_ready, i * BC + c + 1)
                        if q < 2:
                            nc.scalar.activation(hid1[:, h, :], mlp_ps[:, h, :], ACT.Silu, bias=b1_col[:]).then_inc(silu_done, 1)
                        else:
                            if q == 2:
                                act.wait_ge(stored[s], i * 16 + 16)
                            nc.scalar.activation(hid2[:, s, h * 512:(h + 1) * 512], mlp_ps[:, h, :], ACT.Silu,
                                                 bias=b2_col[:]).then_inc(silu_done, 1)
                        if q == 3:
                            act.wait_ge(silu_done, i * BC + c + 1 + 2)
                            act.dma_start(hidden[bass.ds(g2 * 2 + s, 1), :, :].rearrange("a p c -> (a p) c"),
                                          hid2[:, s, :]).then_inc(stored[s], 16)
                        if c:
                            copy_sums(i, c - 1)
                    copy_sums(i, BC - 1)
                for s in range(2):
                    act.wait_ge(stored[s], R * (G2 * 16) + 16)
                    act.sem_inc(passed, 1)

            @block.vector
            def _(dve):
                dve.sem_inc(msg_ready, AHEAD)
                dve.sem_inc(rows_read, 2)
                R = dve.value_load(rounds[0:1, 0:1], min_val=1, max_val=RM)
                LINKS = 2 * (2 + 5 * CH)
                with dve.Fori(0, R) as r, dve.Fori(0, G2) as g2:
                    i = r * G2 + g2
                    link = 0
                    for c in range(BC):
                        s, q = divmod(c, CH)
                        dve.wait_ge(msg_ready, i * BC + c + AHEAD)
                        if q == 0:
                            dve.wait_ge(l0_in[s], (i + 1) * (16 * L0_LOADS))
                            nc.vector.tensor_tensor(node_col[:], iota_col[:], base_in[:, s:s + 1], ALU.add)
                            nc.vector.tensor_copy(src_f[:], src_i[:, s, :]).then_inc(link0, 1)
                            link += 1
                            dve.wait_ge(link0, i * LINKS + link)
                            nc.vector.tensor_scalar(to_spare[:], src_f[:], -1.0, spare_col[:], ALU.mult, ALU.add).then_inc(link0, 1)
                            link += 1
                            dve.wait_ge(link0, i * LINKS + link)
                        dve.wait_ge(rows_ready, i * BC + c + 1)
                        nc.vector.tensor_scalar(pick[:, c % 2, :, :].rearrange("p t e -> p (t e)"), rows_ps[:, c % 2, 0, :],
                                                node_col[:], None, ALU.is_equal).then_inc(pick_ready, 1)
                        dve.wait_ge(merged, i * BC + c - 1 + AHEAD)
                        for t in range(CT):
                            last = nc.vector.scalar_tensor_tensor(
                                same[:, c % 2, t, :], rows_ps[:, c % 2, 1, t * P:(t + 1) * P],
                                src_f[:, q * CT + t:q * CT + t + 1], upper[:], ALU.is_equal, ALU.mult,
                                accum_out=later[:, t:t + 1])
                        last.then_inc(rows_read, 1)
                        dve.wait_ge(rows_read, i * BC + c + 1 + 2)
                        nc.vector.scalar_tensor_tensor(hop[:], later[:], 1.5, to_spare[:, q * CT:(q + 1) * CT],
                                                       ALU.is_gt, ALU.mult).then_inc(link0, 1)
                        link += 1
                        dve.wait_ge(link0, i * LINKS + link)
                        dve.wait_ge(landed, i * (2 * TILES) + c * CT + 1)
                        nc.vector.tensor_tensor(where[:, s, q * CT:(q + 1) * CT], src_f[:, q * CT:(q + 1) * CT], hop[:],
                                                ALU.add).then_inc(where_ready, 1)
                        dve.wait_ge(picked, i * BC + c + 1)
                        nc.vector.tensor_tensor(msg[:], picks, w_sb[:, s, q * CT:(q + 1) * CT].unsqueeze(2).to_broadcast([P, CT, FW]),
                                                ALU.mult).then_inc(link0, 1)
                        m = msg_b[:, c % 2]
                        dve.wait_ge(link0, i * LINKS + link + 1)
                        nc.vector.tensor_copy(m[:, 0], msg[:]).then_inc(link0, 1)
                        dve.wait_ge(link0, i * LINKS + link + 2)
                        nc.vector.tensor_tensor(left[:], msg[:], m[:, 0], ALU.subtract).then_inc(link0, 1)
                        dve.wait_ge(link0, i * LINKS + link + 3)
                        nc.vector.tensor_copy(m[:, 1], left[:]).then_inc(link0, 1)
                        link += 4
                        dve.wait_ge(link0, i * LINKS + link)
                        nc.vector.tensor_tensor(m[:, 2], left[:], m[:, 1], ALU.subtract).then_inc(msg_ready, 1)

            @block.gpsimd
            def _(pool):
                pool.sem_inc(landed, LANDED_AHEAD)
                R = pool.value_load(rounds[0:1, 0:1], min_val=1, max_val=RM)
                with pool.Fori(0, R) as r, pool.Fori(0, G2) as g2:
                    i = r * G2 + g2
                    for t in range(2 * TILES):
                        c = t // CT
                        if t % CT == 0:
                            pool.wait_ge(where_ready, i * BC + c + 1)
                            pool.wait_ge(sums_ready, i * BC + c + 1 + 2)
                        pool.wait_ge(added[t % NTAB], i * (16 * ADDS) + 16 * (t // NTAB) + 16)
                        pool.sem_inc(landed, 1)
                        s, u = divmod(t, TILES)
                        pool.indirect_dma_start(
                            lap_tab[t % NTAB], bass.IndirectOffsetOnAxis(ap=where[:, s, u:u + 1], axis=0),
                            sums[:, s, u, :], None, compute_op=ALU.add).then_inc(added[t % NTAB], 16)
                for k in range(NTAB):
                    pool.wait_ge(added[k], R * (G2 * 16 * ADDS) + 16)
                    pool.sem_inc(passed, 1)

        win_out = sem("win_out")
        laps_in, self_t, self_c, self_ready, agg_ready = sem("laps_in"), sem("self_t"), sem("self_c"), sem("self_ready"), sem("agg_ready")
        centered2, squared2, var_ready2, std_ready2, h2_ready, nodes_out = (
            sem("centered2"), sem("squared2"), sem("var_ready2"), sem("std_ready2"), sem("h2_ready"), sem("nodes_out"))

        mid = ExitStack()
        with mid:
            laps = [sb(mid, f"laps{k}", [NP, C, FW]) for k in range(NTAB)]
            mean = sb(mid, "mean2", [NP, C])
            std = sb(mid, "std2", [NP, C])
            h2_sb = sb(mid, "h2_sb", [NP, C * F])
            h2_t = sb(mid, "h2_t", [P, 2, 4, NP])
            t_ps = pb(mid, "t_ps", [P, 2, 512])
            self_ps = pb(mid, "self_ps", [P, 2, 512])
            xc = laps[1][:, :, 0:F]
            sq = laps[2][:, :, 0:F]
            quads = C * F // P
            batches = [range(k, min(k + 4, quads)) for k in range(0, quads, 4)]
            block = mid.enter_context(nc.Block("nodes"))

            @block.sync
            def _(sp):
                for k in range(NTAB):
                    sp.dma_start(laps[k][:].rearrange("p c f -> p (c f)"),
                                 lap_tab[k][0:N, :].rearrange("(p c) f -> p (c f)", p=NP)).then_inc(laps_in, 16)
                sp.dma_start(hidden[G], hidden[0]).then_inc(nodes_out, 16)
                sp.wait_ge(h2_ready, 1)
                sp.dma_start(h2_tab[0:N, :].rearrange("(p c) f -> p (c f)", p=NP), h2_sb[:]).then_inc(nodes_out, 16)
                sp.wait_ge(agg_ready, len(batches))
                sp.dma_start(agg_tab[0:N, :].rearrange("(p c) f -> p (c f)", p=NP),
                             x_sb[:].rearrange("p c f -> p (c f)")).then_inc(win_out, 16)
                sp.wait_ge(nodes_out, 32)
                sp.wait_ge(win_out, 16)

            @block.vector
            def _(dve):
                dve.wait_ge(laps_in, 16 * NTAB)
                half = NTAB
                while half > 1:
                    half //= 2
                    for k in range(half):
                        last = nc.vector.tensor_tensor(laps[k][:], laps[k][:], laps[k + half][:], ALU.add)
                    then(dve, last)
                then(dve, nc.vector.tensor_tensor(laps[1][:, :, 0:F], h1_sb[:, :, 0:F],
                                                  laps[0][:, :, F:FW].to_broadcast([NP, C, F]), ALU.mult))
                then(dve, nc.vector.tensor_tensor(laps[0][:, :, 0:F], laps[0][:, :, 0:F], laps[1][:, :, 0:F], ALU.subtract))
                then(dve, nc.vector.tensor_tensor(x_sb[:], x_sb[:], laps[0][:, :, 0:F], ALU.add))
                center(dve, x_sb[:], mean, xc, centered2)
                normalise(dve, sq, mean, std, xc, h2_sb[:].rearrange("p (c f) -> p c f", f=F),
                          squared2, var_ready2, std_ready2, h2_ready)
                flat = x_sb[:].rearrange("p c f -> p (c f)")
                for b, quad in enumerate(batches):
                    dve.wait_ge(self_ready, b + 1)
                    cols = flat[:, quad[0] * P:(quad[-1] + 1) * P]
                    nc.vector.scalar_tensor_tensor(cols, self_ps[0:NP, b % 2, 0:len(quad) * P], SELF_SCALE, cols,
                                                   ALU.mult, ALU.add).then_inc(agg_ready, 1)

            @block.scalar
            def _(act):
                act.wait_ge(centered2, 1)
                nc.scalar.activation(sq, xc, ACT.Square).then_inc(squared2, 1)
                act.wait_ge(var_ready2, 1)
                nc.scalar.activation(std[:], mean[:], ACT.Sqrt, scale=1.0 / F, bias=eps_col[0:NP, :]).then_inc(std_ready2, 1)
                for b, quad in enumerate(batches):
                    act.wait_ge(self_t, b + 1)
                    if b >= 2:
                        act.wait_ge(self_ready, b - 1)
                    nc.scalar.activation(h2_t[:, b % 2, 0:len(quad), :],
                                         t_ps[:, b % 2, 0:len(quad) * NP].rearrange("p (q n) -> p q n", n=NP),
                                         ACT.Copy).then_inc(self_c, 1)

            @block.tensor
            def _(pe):
                pe.wait_ge(h2_ready, 1)
                for b, quad in enumerate(batches):
                    if b >= 2:
                        pe.wait_ge(self_c, b - 1)
                    for k, q in enumerate(quad):
                        last = nc.tensor.transpose(t_ps[:, b % 2, k * NP:(k + 1) * NP], h2_sb[:, q * P:(q + 1) * P],
                                                   ident[0:NP, 0:NP])
                    last.then_inc(self_t, 1)
                    pe.wait_ge(self_c, b + 1)
                    if b >= 2:
                        pe.wait_ge(agg_ready, b - 1)
                    for k, q in enumerate(quad):
                        last = nc.tensor.matmul(self_ps[0:NP, b % 2, k * P:(k + 1) * P], h2_t[:, b % 2, k, :], self_bd[:],
                                                start=True, stop=True)
                    last.then_inc(self_ready, 1)

        L1_LOADS = 5
        DONE = BC
        l1_in = [sem("l1_in0"), sem("l1_in1")]
        got = [sem(f"got{c}") for c in range(BC)]
        delta_ready, onehot_ready, scaled_ready = sem("delta_ready"), sem("onehot_ready"), sem("scaled_ready")
        paths_ready, parts_ready, agg_done, acc_read = sem("paths_ready"), sem("parts_ready"), sem("agg_done"), sem("acc_read")
        win_in, win_ready = sem("win_in"), sem("win_ready")
        link1, sq_step = sem("link1"), sem("sq_step")
        ones_ready = sem("ones_ready")

        lay1 = ExitStack()
        with lay1:
            hid_sb = sb(lay1, "hid_sb", [HR + 1, 2, GE])
            idx_sb = sb(lay1, "idx_sb", [P, 2, TILES], i32)
            dst_sb = sb(lay1, "dst_sb", [P, 2, TILES], i32)
            sh_sb = sb(lay1, "sh_sb", [P, 2, TILES, 4])
            base_sb1 = sb(lay1, "base_sb1", [P, 2])
            delta = sb(lay1, "delta", [P, 2, TILES])
            hs = sb(lay1, "hs", [P, 2, TILES, F])
            dist = sb(lay1, "dist", [P, CT, P])
            onehot = sb(lay1, "onehot", [P, 2, CT, P])
            scaled = sb(lay1, "scaled", [P, 2, CT, F + MUL])
            vsh = sb(lay1, "vsh", [P, CT, MUL, 3])
            prod01 = sb(lay1, "prod01", [P, CT, MUL, MUL])
            prod10 = sb(lay1, "prod10", [P, CT, 3, MUL * MUL])
            vec0 = sb(lay1, "vec0", [P, CT, MUL])
            parts = sb(lay1, "parts", [P, 2, CT, RC])
            red = sb(lay1, "red", [P, F])
            win_old = sb(lay1, "win_old", [P, F])
            win_new = sb(lay1, "win_new", [P, F])
            paths_ps = pb(lay1, "paths_ps", [P, 2, CT, WN])
            acc_ps = pb(lay1, "acc_ps", [P, 2, 512])
            m2 = MUL * MUL

            block = lay1.enter_context(nc.Block("layer1"))

            @block.sync
            def _(sp):
                R = sp.value_load(rounds[0:1, 0:1], min_val=1, max_val=RM)

                def load(s, r, g):
                    for h in range(2):
                        sp.dma_start(hid_sb[0:HR, s, h * HALF:(h + 1) * HALF],
                                     hidden[bass.ds(g, 1), h * HR:(h + 1) * HR, :].rearrange("a p c -> (a p) c")).then_inc(l1_in[s], 16)
                    sp.dma_start(idx_sb[:, s, :], src_col[:, bass.ds(g * TILES, TILES)]).then_inc(l1_in[s], 16)
                    sp.dma_start(dst_sb[:, s, :], dst_col[:, bass.ds(g * TILES, TILES)]).then_inc(l1_in[s], 16)
                    sp.dma_start(sh_sb[:, s, :, :].rearrange("p t c -> p (t c)"),
                                 sh_col[:, bass.ds(g * (TILES * 4), TILES * 4)]).then_inc(l1_in[s], 16)
                    sp.dma_start(base_sb1[:, s:s + 1], base_f[:, bass.ds(r * BW + g + 1, 1)].to_broadcast([P, 1]),
                                 allow_slow_non_contiguous=True).then_inc(l1_in[s], 16)

                def add_window(n, at):
                    sp.wait_ge(win_out, n * 16 + 16)
                    sp.sem_inc(passed, 1)
                    base = sp.value_load(base_i[:, bass.ds(at, 1)], min_val=0, max_val=NT - P)
                    sp.dma_start(win_old[:], agg_tab[bass.ds(base, P), :]).then_inc(win_in, 16)
                    sp.wait_ge(win_ready, n + 1)
                    sp.dma_start(agg_tab[bass.ds(base, P), :], win_new[:]).then_inc(win_out, 16)

                zero = sp.snap(R * 0)
                load(0, zero, zero)
                with sp.Fori(0, R) as r, sp.Fori(0, G2) as g2:
                    i = r * G2 + g2
                    for s in range(2):
                        n, g = i * 2 + s, g2 * 2 + s
                        sp.wait_ge(parts_ready, n * CH + DONE)
                        load(1 - s, r, g + 1)
                        add_window(n, r * BW + g)
                add_window(R * G, (R - 1) * BW + G)
                sp.wait_ge(win_out, (R * G + 2) * 16)
                sp.wait_ge(l1_in[0], (R * G2 + 1) * (16 * (L1_LOADS + 1)))
                sp.sem_inc(passed, 1)

            @block.gpsimd
            def _(pool):
                R = pool.value_load(rounds[0:1, 0:1], min_val=1, max_val=RM)
                with pool.Fori(0, R) as r, pool.Fori(0, G2) as g2:
                    i = r * G2 + g2
                    for c in range(BC):
                        s, q = divmod(c, CH)
                        if q == 0:
                            pool.wait_ge(l1_in[s], (i + 1) * (16 * (L1_LOADS + 1)))
                        pool.wait_ge(parts_ready, i * BC + c + 1)
                        pool.sem_inc(passed, 1)
                        for t in range(q * CT, (q + 1) * CT):
                            pool.indirect_dma_start(hs[:, s, t, :], None, h2_tab,
                                                    bass.IndirectOffsetOnAxis(ap=idx_sb[:, s, t:t + 1], axis=0)).then_inc(got[c], 16)

            @block.scalar
            def _(act):
                act.sem_inc(onehot_ready, 1)
                R = act.value_load(rounds[0:1, 0:1], min_val=1, max_val=RM)
                with act.Fori(0, R) as r, act.Fori(0, G2) as g2:
                    i = r * G2 + g2
                    for c in range(BC):
                        s, q = divmod(c, CH)
                        act.wait_ge(got[c], (i + 1) * (16 * CT))
                        act.wait_ge(parts_ready, i * BC + c - 1 + DONE)
                        for t in range(CT):
                            last = nc.scalar.activation(scaled[:, c % 2, t, MUL:MUL + F], hs[:, s, q * CT + t, :], ACT.Copy,
                                                        scale=sh_sb[:, s, q * CT + t, 0:1])
                        last.then_inc(scaled_ready, 1)
                        act.wait_ge(onehot_ready, i * BC + c + 1)
                        act.wait_ge(delta_ready, i * 2 + s + 1)
                        for t in range(CT):
                            last = nc.scalar.activation(dist[:, t, :], iota_row[:], ACT.Square,
                                                        bias=delta[:, s, q * CT + t:q * CT + t + 1])
                        last.then_inc(sq_step, 1)
                        act.wait_ge(sq_step, i * BC + c + 1)
                        act.wait_ge(agg_done, i * BC + c + 1)
                        nc.scalar.activation(onehot[:, c % 2, :, :].rearrange("p t e -> p (t e)"),
                                             dist[:].rearrange("p t e -> p (t e)"),
                                             ACT.Relu, scale=-2.0, bias=1.0).then_inc(onehot_ready, 1)

            @block.tensor
            def _(pe):
                pe.sem_inc(agg_done, 2)
                R = pe.value_load(rounds[0:1, 0:1], min_val=1, max_val=RM)
                pe.wait_ge(ones_ready, 1)

                def path_weights(i, c):
                    s, q = divmod(c % BC, CH)
                    if q == 0:
                        pe.wait_ge(l1_in[s], (i + c // BC + 1) * (16 * (L1_LOADS + 1)))
                    pe.wait_ge(parts_ready, i * BC + c - 1 + DONE)
                    for t in range(CT):
                        e = (q * CT + t) * P
                        last = nc.tensor.matmul(paths_ps[:, c % 2, t, :], hid_sb[:, s, e:e + P], w3_sb[:], start=True, stop=True)
                    last.then_inc(paths_ready, 1)

                def aggregate(i, c):
                    s, q = divmod(c, CH)
                    pe.wait_ge(onehot_ready, i * BC + c + 2)
                    pe.wait_ge(parts_ready, i * BC + c + 1 + DONE)
                    if q == 0:
                        pe.wait_ge(acc_read, i * 2 + s + 1)
                    for t in range(CT):
                        last = nc.tensor.matmul(acc_ps[:, s, 0:RC], onehot[:, c % 2, t, :], parts[:, c % 2, t, :],
                                                start=(q == 0 and t == 0), stop=(q == CH - 1 and t == CT - 1))
                    last.then_inc(agg_done, 1)

                path_weights(0, 0)
                with pe.Fori(0, R) as r, pe.Fori(0, G2) as g2:
                    i = r * G2 + g2
                    for c in range(BC):
                        path_weights(i, c + 1)
                        if c:
                            aggregate(i, c - 1)
                    aggregate(i, BC - 1)

            @block.vector
            def _(dve):
                dve.sem_inc(parts_ready, DONE)
                dve.sem_inc(acc_read, 1)
                nc.vector.memset(hid_sb[HR:HR + 1, :, :], 1.0).then_inc(ones_ready, 1)
                nc.vector.memset(acc_ps[:, 1, 0:RC], 0.0)
                R = dve.value_load(rounds[0:1, 0:1], min_val=1, max_val=RM)

                def add_window(n, s):
                    dve.wait_ge(agg_done, n * CH + 2)
                    nc.vector.tensor_reduce(red[:, 0:MUL], acc_ps[:, s, 0:RS].rearrange("p (u w) -> p w u", w=MUL), axis=AX, op=ALU.add)
                    nc.vector.tensor_reduce(red[:, MUL:F], acc_ps[:, s, RS:RC].rearrange("p (i u w) -> p i w u", i=3, w=MUL),
                                            axis=AX, op=ALU.add).then_inc(acc_read, 1)
                    dve.wait_ge(acc_read, n + 2)
                    dve.wait_ge(win_in, (n + 1) * 16)
                    nc.vector.scalar_tensor_tensor(win_new[:, 0:MUL], red[:, 0:MUL], MSG_SCALE, win_old[:, 0:MUL], ALU.mult, ALU.add)
                    nc.vector.scalar_tensor_tensor(win_new[:, MUL:F].rearrange("p (w i) -> p w i", i=3),
                                                   red[:, MUL:F].rearrange("p (i w) -> p w i", i=3), MSG_SCALE,
                                                   win_old[:, MUL:F].rearrange("p (w i) -> p w i", i=3),
                                                   ALU.mult, ALU.add).then_inc(win_ready, 1)

                with dve.Fori(0, R) as r, dve.Fori(0, G2) as g2:
                    i = r * G2 + g2
                    for c in range(BC):
                        s, q = divmod(c, CH)
                        if q == 0:
                            dve.wait_ge(l1_in[s], (i + 1) * (16 * (L1_LOADS + 1)))
                            nc.vector.tensor_scalar(delta[:, s, :], dst_sb[:, s, :], -1.0, base_sb1[:, s:s + 1],
                                                    ALU.mult, ALU.add).then_inc(delta_ready, 1)
                        tiles = slice(q * CT, (q + 1) * CT)
                        sc, W, out_c = scaled[:, c % 2], paths_ps[:, c % 2], parts[:, c % 2]
                        dve.wait_ge(got[c], (i + 1) * (16 * CT))
                        nc.vector.tensor_tensor(vsh[:], hs[:, s, tiles, MUL:F].rearrange("p t (u i) -> p t u i", i=3),
                                                sh_sb[:, s, tiles, 1:4].unsqueeze(2).to_broadcast([P, CT, MUL, 3]),
                                                ALU.mult).then_inc(link1, 1)
                        dve.wait_ge(paths_ready, i * BC + c + 1)
                        nc.vector.tensor_tensor(prod01[:], W[:, :, 2 * m2:3 * m2].rearrange("p t (u w) -> p t u w", w=MUL),
                                                hs[:, s, tiles, 0:MUL].unsqueeze(3).to_broadcast([P, CT, MUL, MUL]), ALU.mult)
                        dve.wait_ge(link1, i * (3 * BC) + 3 * c + 1)
                        nc.vector.tensor_reduce(sc[:, :, 0:MUL], vsh[:], axis=AX, op=ALU.add).then_inc(link1, 1)
                        dve.wait_ge(scaled_ready, i * BC + c + 1)
                        dve.wait_ge(parts_ready, i * BC + c + DONE)
                        for k in range(3):
                            nc.vector.tensor_tensor(
                                prod10[:, :, k, :].rearrange("p t (u w) -> p t u w", w=MUL),
                                W[:, :, 3 * m2:4 * m2].rearrange("p t (u w) -> p t u w", w=MUL),
                                sc[:, :, 2 * MUL + k:2 * MUL + F - MUL:3].unsqueeze(3).to_broadcast([P, CT, MUL, MUL]), ALU.mult)
                        dve.wait_ge(link1, i * (3 * BC) + 3 * c + 2)
                        nc.vector.tensor_reduce(vec0[:], prod01[:].rearrange("p t u w -> p t w u"), axis=AX,
                                                op=ALU.add).then_inc(link1, 1)
                        dve.wait_ge(agg_done, i * BC + c + 1)
                        nc.vector.tensor_tensor(out_c[:, :, 0:RS].rearrange("p t (k w) -> p t k w", w=MUL),
                                                W[:, :, 0:2 * m2].rearrange("p t (k w) -> p t k w", w=MUL),
                                                sc[:, :, 0:2 * MUL].unsqueeze(3).to_broadcast([P, CT, 2 * MUL, MUL]), ALU.mult)
                        dve.wait_ge(link1, i * (3 * BC) + 3 * c + 3)
                        vec = out_c[:, :, RS:RC].rearrange("p t (i k) -> p t i k", i=3)
                        nc.vector.tensor_tensor(vec[:, :, :, 0:m2 // 2], prod10[:, :, :, 0:m2 // 2], prod10[:, :, :, m2 // 2:m2], ALU.add)
                        nc.vector.tensor_tensor(vec[:, :, :, m2 // 2:SUMS * MUL], vec0[:].unsqueeze(2).to_broadcast([P, CT, 3, MUL]),
                                                sh_sb[:, s, tiles, 1:4].unsqueeze(3).to_broadcast([P, CT, 3, MUL]),
                                                ALU.mult).then_inc(parts_ready, 1)
                        if q == 2:
                            add_window(i * 2 + s, 1 - s)
                add_window(R * G, 1)

        result_out = sem("result_out")
        with ExitStack() as fin:
            block = fin.enter_context(nc.Block("result"))

            @block.sync
            def _(sp):
                sp.dma_start(out.rearrange("(p c) f -> p (c f)", p=P - 3),
                             agg_tab[0:N, :].rearrange("(p c) f -> p (c f)", p=P - 3)).then_inc(result_out, 16)
                sp.wait_ge(result_out, 16)


def laid_out(x, src, dst, edge_attr_4, edge_attr_8, edge_weight, weights):
    import numpy as np
    n, e = x.shape[0], src.shape[0]
    groups = -(-e // GE)
    groups += groups % 2
    pad = groups * GE - e

    def padded(a, v):
        return np.concatenate([a, np.full((pad,) + a.shape[1:], v, a.dtype)])

    def columns(a):
        a = a.reshape(groups * TILES, P, -1).transpose(1, 0, 2)
        a = np.concatenate([a, a[:, :TILES]], axis=1)
        return np.ascontiguousarray(a.reshape(P, -1))

    src, dst = (padded(a.astype(np.int32), n) for a in (src, dst))
    sh, rad, w = padded(edge_attr_4, 0), padded(edge_attr_8, 0), padded(edge_weight, 0)
    rad = np.ascontiguousarray(rad.reshape(groups, 2, HALF, MUL).transpose(0, 1, 3, 2).reshape(groups, 2 * MUL, HALF))
    return dict(x=x, src_row=src, dst_row=dst, src_col=columns(src), dst_col=columns(dst), w_col=columns(w),
                sh_col=columns(sh), radial=rad, **weights)


def kernel(**inputs):
    import numpy as _np
    import concourse.bacc as _bacc
    from concourse import mybir as _mybir
    from concourse.bass_utils import run_bass_kernel_spmd as _run

    a = {k: _np.asarray(v) for k, v in inputs.items()}
    weights = {k: a["L1_gnn_" + k] for k in ("W1", "b1", "W2", "b2", "W3", "b3", "Ws", "Wv")}
    arrays = laid_out(a["x"], a["src"], a["dst"], a["edge_attr_4"], a["edge_attr_8"], a["edge_weight"], weights)
    nc = _bacc.Bacc("TRN2", target_bir_lowering=False, num_devices=1)
    args = {k: nc.dram_tensor(f"in_{k}_dram", v.shape, _mybir.dt.from_np(v.dtype), kind="ExternalInput").ap()
            for k, v in arrays.items()}
    out = nc.dram_tensor("out_dram", a["x"].shape, _mybir.dt.float32, kind="ExternalOutput").ap()
    gnn_program(nc, **args, out=out)
    r = _run(nc, [{f"in_{k}_dram": _np.ascontiguousarray(v) for k, v in arrays.items()}], core_ids=[0])
    return r.results[0]["out_dram"]
```

```python
import concourse.bass as bass
from concourse import mybir
from contextlib import ExitStack
from math import sqrt

P = 128
F = 32
MUL = 8
FW = F + 1
PARTS = 3
TILES = 16
GE = TILES * P
HALF = GE // 2
CT = 4
CH = TILES // CT
BC = 2 * CH
NTAB = 8
EARLY = 5
HR = 64
WN = 4 * MUL * MUL
SUMS = 5
RS = 2 * MUL * MUL
RC = RS + 3 * SUMS * MUL
NP = 125
EPS = 1e-5
AVG_NEI = 16.0
MSG_SCALE = 1.0 / sqrt(2.0 * MUL) / sqrt(AVG_NEI)
SELF_SCALE = 1.0 / sqrt(MUL)


def rounds_of(n_nodes):
    return -(-(n_nodes + 1) // P)


def table_rows(n_nodes):
    return max(-(-(n_nodes + 1 + P) // P), rounds_of(n_nodes) + 1) * P


def gnn_program(nc, x, src_row, dst_row, src_col, dst_col, w_col, sh_col, radial,
                W1, b1, W2, b2, W3, b3, Ws, Wv, out):
    f32, bf16, i32 = mybir.dt.float32, mybir.dt.bfloat16, mybir.dt.int32
    ALU, ACT, AX = mybir.AluOpType, mybir.ActivationFunctionType, mybir.AxisListType.X
    N = x.shape[0]
    G = radial.shape[0]
    G2 = G // 2
    RM, NT = rounds_of(N), table_rows(N)
    C = N // NP
    CE = G * GE // P
    TAIL = NT - N
    BW = G + 2

    def table(name, shape, dt=f32):
        return nc.dram_tensor(name, shape, dt, kind="Internal").ap()

    h1_tab = table("h1_tab", (NT, PARTS * FW), bf16)
    h2_tab = table("h2_tab", (NT, F))
    agg_tab = table("agg_tab", (NT, F))
    lap_tab = [table(f"lap_tab{k}", (NT, FW)) for k in range(NTAB)]
    digits = table("digits", (2, 2, G * GE), bf16)
    hidden = table("hidden", (G + 1, P, HALF))
    base_f = table("base_f", (1, RM * BW))
    base_i = table("base_i", (1, RM * BW), i32)

    whole = ExitStack()
    with whole:
        def sb(ctx, name, shape, dt=f32):
            return ctx.enter_context(nc.sbuf_tensor(name, shape, dt))

        def pb(ctx, name, shape, dt=f32):
            return ctx.enter_context(nc.psum_tensor(name, shape, dt))

        def sem(name):
            return whole.enter_context(nc.semaphore(name))

        iota_row = sb(whole, "iota_row", [P, P])
        iota_col = sb(whole, "iota_col", [P, 1])
        spare_col = sb(whole, "spare_col", [P, 1])
        ident = sb(whole, "ident", [P, P])
        upper = sb(whole, "upper", [P, P])
        x_sb = sb(whole, "x_sb", [NP, C, F])
        h1_sb = sb(whole, "h1_sb", [NP, C, FW])
        w1_bd = sb(whole, "w1_bd", [2 * MUL, P])
        w2_bd = sb(whole, "w2_bd", [P, P])
        b1_col = sb(whole, "b1_col", [P, 1])
        b2_col = sb(whole, "b2_col", [P, 1])
        w3_sb = sb(whole, "w3_sb", [HR + 1, WN])
        self_bd = sb(whole, "self_bd", [P, P])
        place_val = sb(whole, "place_val", [2, P], bf16)
        rounds = sb(whole, "rounds", [1, 1], i32)
        eps_col = sb(whole, "eps_col", [P, 1])
        zeros = sb(whole, "zeros", [P, max(NT // P, TAIL // 4) * FW])

        dve_step = sem("dve_step")
        passed = sem("passed")
        steps = {"dve": 0}

        def then(dve, ins):
            steps["dve"] += 1
            ins.then_inc(dve_step, 1)
            dve.wait_ge(dve_step, steps["dve"])

        def center(dve, rows, mean, xc, centered):
            then(dve, nc.vector.tensor_reduce(mean, rows, axis=AX, op=ALU.add))
            then(dve, nc.vector.tensor_scalar(mean, mean, 1.0 / F, None, ALU.mult))
            nc.vector.tensor_tensor(xc, rows, mean.unsqueeze(2).to_broadcast(list(rows.shape)),
                                    ALU.subtract).then_inc(centered, 1)

        def normalise(dve, std, xc, normed, h_ready):
            then(dve, nc.vector.reciprocal(std, std))
            nc.vector.scalar_tensor_tensor(normed, xc, 0.0, std.unsqueeze(2).to_broadcast(list(xc.shape)),
                                           ALU.max, ALU.mult).then_inc(h_ready, 1)

        x_in, idx_in, rows_in, w_in = sem("x_in"), sem("idx_in"), sem("rows_in"), sem("w_in")
        iota_done, cleared, zero_ready = sem("iota_done"), sem("cleared"), sem("zero_ready")
        first_ready, first_seen, bad_ready, bad_seen = sem("first_ready"), sem("first_seen"), sem("bad_ready"), sem("bad_seen")
        split = [sem("split_dst"), sem("split_src")]
        centered, squared, var_ready, std_ready, h1_ready, rest_ready = (
            sem("centered"), sem("squared"), sem("var_ready"), sem("std_ready"), sem("h1_ready"), sem("rest_ready"))
        part_ready, digits_seen = sem("part_ready"), sem("digits_seen")
        added = [sem(f"added{k}") for k in range(NTAB)]
        base_ready, sp_out, act_out = sem("base_ready"), sem("sp_out"), sem("act_out")

        def clear_table(pool, k):
            pool.dma_start(lap_tab[k].rearrange("(p c) f -> p (c f)", p=P),
                           zeros[:, 0:NT // P * FW]).then_inc(added[k], 16)

        prep = ExitStack()
        with prep:
            iota_i = sb(prep, "iota_i", [P, P + 1], i32)
            ones = sb(prep, "ones", [P, P])
            zeros_b = sb(prep, "zeros_b", [4, TAIL // 4 * PARTS * FW], bf16)
            row_i = [sb(prep, f"row_i{a}", [P, CE], i32) for a in range(2)]
            high_i = [sb(prep, f"high_i{a}", [P, CE], i32) for a in range(2)]
            digit_b = sb(prep, "digit_b", [P, 2, 2, CE], bf16)
            first_i = sb(prep, "first_i", [1, G], i32)
            first_f = sb(prep, "first_f", [1, G])
            dst_i = sb(prep, "dst_i", [P, G, TILES], i32)
            off = sb(prep, "off", [P, G, TILES])
            ext = sb(prep, "ext", [P, 2])
            bad = sb(prep, "bad", [P, 1])
            sel = sb(prep, "sel", [P, 5])
            base_sb = sb(prep, "base_sb", [P, BW])
            base_isb = sb(prep, "base_isb", [P, BW], i32)
            mean = sb(prep, "mean", [NP, C])
            std = sb(prep, "std", [NP, C])
            rest = sb(prep, "rest", [NP, C, FW])
            sq = rest[:, :, 0:F]
            xc = sb(prep, "xc", [NP, C, F])
            w3_raw = sb(prep, "w3_raw", [HR + 1, WN])
            first_ps = pb(prep, "first_ps", [P, 512])
            bad_ps = pb(prep, "bad_ps", [P, 512])
            h1_b = sb(prep, "h1_b", [NP, C, PARTS, FW], bf16)
            W_LOADS = 4 * 2 + 2 + 4 * 4

            block = prep.enter_context(nc.Block("prepare"))

            @block.sync
            def _(sp):
                sp.dma_start(x_sb[:].rearrange("p c f -> p (c f)"),
                             x.rearrange("(p c) f -> p (c f)", p=NP)).then_inc(x_in, 16)
                sp.dma_start(dst_i[:].rearrange("p g t -> p (g t)"), dst_col[:, 0:G * TILES]).then_inc(idx_in, 16)
                sp.dma_start(first_i[:], dst_row.rearrange("(a g e) -> a g e", a=1, e=GE)[:, :, 0],
                             allow_slow_non_contiguous=True).then_inc(idx_in, 16)
                for a, row in enumerate((dst_row, src_row)):
                    sp.dma_start(row_i[a][:], row.rearrange("(p c) -> p c", p=P)).then_inc(rows_in, 16)
                for a in range(2):
                    sp.wait_ge(split[a], 2)
                    for d in range(2):
                        sp.dma_start(digits[d, a].rearrange("(p c) -> p c", p=P), digit_b[:, d, a, :]).then_inc(sp_out, 16)
                sp.wait_ge(part_ready, PARTS)
                sp.dma_start(h1_tab[0:N, :].rearrange("(p c) f -> p (c f)", p=NP),
                             h1_b[:].rearrange("p c k f -> p (c k f)")).then_inc(sp_out, 16)
                sp.wait_ge(base_ready, 2)
                sp.dma_start(base_f.rearrange("a (r g) -> (a r) g", g=BW), base_sb[0:RM, :]).then_inc(sp_out, 16)
                sp.dma_start(base_i.rearrange("a (r g) -> (a r) g", g=BW), base_isb[0:RM, :]).then_inc(sp_out, 16)
                sp.wait_ge(sp_out, 16 * 7)

            @block.gpsimd
            def _(pool):
                nc.gpsimd.iota(iota_i[:, 0:P], pattern=[[1, P]], base=0, channel_multiplier=0).then_inc(iota_done, 1)
                nc.gpsimd.iota(iota_i[:, P:P + 1], pattern=[[1, 1]], base=0, channel_multiplier=1).then_inc(iota_done, 1)
                for tile in (w1_bd, w2_bd, self_bd):
                    nc.gpsimd.memset(tile[:], 0.0).then_inc(cleared, 1)
                nc.gpsimd.memset(ones[:], 1.0).then_inc(cleared, 1)
                nc.gpsimd.memset(eps_col[:], EPS).then_inc(cleared, 1)
                nc.gpsimd.memset(zeros_b[:], 0.0)
                nc.gpsimd.memset(zeros[:], 0.0).then_inc(zero_ready, 1)
                pool.wait_ge(zero_ready, 1)
                for k in range(EARLY):
                    clear_table(pool, k)

            @block.scalar
            def _(act):
                act.wait_ge(cleared, 5)
                for k in range(2):
                    act.dma_start(w1_bd[MUL * k:MUL * k + MUL, HR * k:HR * k + HR], W1).then_inc(w_in, 16)
                    act.dma_start(w2_bd[HR * k:HR * k + HR, HR * k:HR * k + HR], W2).then_inc(w_in, 16)
                    act.dma_start(b1_col[HR * k:HR * k + HR, :], b1.rearrange("(p a) -> p a", a=1)).then_inc(w_in, 16)
                    act.dma_start(b2_col[HR * k:HR * k + HR, :], b2.rearrange("(p a) -> p a", a=1)).then_inc(w_in, 16)
                act.dma_start(w3_raw[0:HR, :], W3).then_inc(w_in, 16)
                act.dma_start(w3_raw[HR:HR + 1, :], b3.rearrange("(a n) -> a n", a=1)).then_inc(w_in, 16)
                for k in range(4):
                    o = F * k
                    act.dma_start(self_bd[o:o + MUL, o:o + MUL], Ws).then_inc(w_in, 16)
                    for i in range(3):
                        v = o + MUL + i
                        act.dma_start(self_bd[v:o + F:3, v:o + F:3], Wv, allow_slow_non_contiguous=True).then_inc(w_in, 16)
                act.wait_ge(centered, 1)
                nc.scalar.activation(sq, xc[:], ACT.Square).then_inc(squared, 1)
                act.wait_ge(var_ready, 1)
                nc.scalar.activation(std[:], mean[:], ACT.Sqrt, scale=1.0 / F, bias=eps_col[0:NP, :]).then_inc(std_ready, 1)

                def round_digits(a):
                    for d in range(2):
                        act.wait_ge(digits_seen, 2 * a + d + 1)
                        nc.scalar.activation(digit_b[:, d, a, :], (high_i, row_i)[d][a][:], ACT.Copy).then_inc(split[a], 1)

                round_digits(0)
                act.wait_ge(h1_ready, 1)
                nc.scalar.activation(h1_b[:, :, 0, :], h1_sb[:], ACT.Copy).then_inc(part_ready, 1)
                round_digits(1)
                act.wait_ge(rest_ready, 1)
                nc.scalar.activation(h1_b[:, :, 1, :], rest[:], ACT.Copy).then_inc(part_ready, 1)
                act.wait_ge(zero_ready, 1)
                act.dma_start(h1_tab[N:NT, :].rearrange("(p c) f -> p (c f)", p=4),
                              zeros_b[:]).then_inc(act_out, 16)
                for tab in (h2_tab, agg_tab):
                    act.dma_start(tab[N:NT, :].rearrange("(p c) f -> p (c f)", p=4),
                                  zeros[0:4, 0:TAIL // 4 * F]).then_inc(act_out, 16)
                act.wait_ge(act_out, 16 * 3)

            @block.tensor
            def _(pe):
                pe.wait_ge(cleared, 5)
                pe.wait_ge(first_ready, 1)
                nc.tensor.matmul(first_ps[:, 0:G], ones[0:1, :], first_f[:], start=True, stop=True).then_inc(first_seen, 1)
                pe.wait_ge(bad_ready, 1)
                nc.tensor.matmul(bad_ps[:, 0:1], ones[:], bad[:], start=True, stop=True).then_inc(bad_seen, 1)

            @block.vector
            def _(dve):
                dve.wait_ge(iota_done, 2)
                nc.vector.tensor_copy(iota_row[:], iota_i[:, 0:P])
                then(dve, nc.vector.tensor_copy(iota_col[:], iota_i[:, P:P + 1]))
                nc.vector.tensor_scalar(upper[:], iota_row[:], iota_col[:], None, ALU.is_ge)
                nc.vector.tensor_scalar(ident[:], iota_row[:], iota_col[:], None, ALU.is_equal)
                nc.vector.tensor_scalar(spare_col[:], iota_col[:], float(N + 1), None, ALU.add)
                then(dve, nc.vector.tensor_scalar(sel[:, 0:1], iota_col[:], float(1 - P), float(P), ALU.mult, ALU.add))
                nc.vector.tensor_scalar(place_val[:], iota_row[0:2, :], 0.0, sel[0:2, 0:1], ALU.mult, ALU.add)
                nc.vector.memset(h1_sb[:, :, F:FW], 1.0)
                dve.wait_ge(x_in, 16)
                center(dve, x_sb[:], mean[:], xc[:], centered)
                dve.wait_ge(idx_in, 32)
                nc.vector.tensor_copy(first_f[:], first_i[:]).then_inc(first_ready, 1)

                def split_digits(a):
                    nc.vector.tensor_single_scalar(high_i[a][:], row_i[a][:], 7, op=ALU.logical_shift_right).then_inc(digits_seen, 1)
                    dve.wait_ge(digits_seen, 2 * a + 1)
                    nc.vector.tensor_single_scalar(row_i[a][:], row_i[a][:], P - 1, op=ALU.bitwise_and).then_inc(digits_seen, 1)

                dve.wait_ge(rows_in, 32)
                split_digits(0)
                dve.wait_ge(squared, 1)
                nc.vector.tensor_reduce(mean[:], sq, axis=AX, op=ALU.add).then_inc(var_ready, 1)
                split_digits(1)
                dve.wait_ge(std_ready, 1)
                normalise(dve, std[:], xc[:], h1_sb[:, :, 0:F], h1_ready)
                dve.wait_ge(first_seen, 1)
                then(dve, nc.vector.tensor_tensor(off[:], dst_i[:], first_ps[:, 0:G].unsqueeze(2).to_broadcast([P, G, TILES]),
                                                  ALU.subtract))
                dve.wait_ge(part_ready, 1)
                nc.vector.tensor_tensor(rest[:], h1_sb[:], h1_b[:, :, 0, :], ALU.subtract).then_inc(rest_ready, 1)
                nc.vector.tensor_reduce(ext[:, 0:1], off[:].rearrange("p g t -> p (g t)"), axis=AX, op=ALU.max)
                then(dve, nc.vector.tensor_reduce(ext[:, 1:2], off[:].rearrange("p g t -> p (g t)"), axis=AX, op=ALU.min))
                nc.vector.tensor_scalar(ext[:, 0:1], ext[:, 0:1], float(P - 1), None, ALU.is_gt)
                then(dve, nc.vector.tensor_scalar(ext[:, 1:2], ext[:, 1:2], 0.0, None, ALU.is_lt))
                nc.vector.tensor_tensor(bad[:], ext[:, 0:1], ext[:, 1:2], ALU.add).then_inc(bad_ready, 1)
                dve.wait_ge(part_ready, 2)
                nc.vector.tensor_tensor(h1_b[:, :, 2, :], rest[:], h1_b[:, :, 1, :], ALU.subtract).then_inc(part_ready, 1)
                dve.wait_ge(bad_seen, 1)
                then(dve, nc.vector.tensor_scalar(sel[:, 0:1], bad_ps[:, 0:1], 1.0, None, ALU.min))
                nc.vector.tensor_scalar(sel[:, 1:2], sel[:, 0:1], -1.0, 1.0, ALU.mult, ALU.add)
                nc.vector.tensor_scalar(rounds[:], sel[0:1, 0:1], float(RM - 1), 1.0, ALU.mult, ALU.add)
                nc.vector.tensor_scalar(sel[:, 2:3], iota_col[:], float(P), None, ALU.mult)
                nc.vector.tensor_scalar(sel[:, 4:5], iota_col[:], float(P), float(P), ALU.mult, ALU.add)
                then(dve, nc.vector.tensor_scalar(sel[:, 3:4], iota_col[:], -1.0, 0.0, ALU.add, ALU.max))
                then(dve, nc.vector.tensor_scalar(sel[:, 3:4], sel[:, 3:4], float(P), None, ALU.mult))
                then(dve, nc.vector.tensor_scalar(sel[:, 2:5], sel[:, 2:5], sel[:, 0:1], None, ALU.mult))
                for cols, of, s in ((slice(1, G + 1), slice(0, G), 2), (slice(0, 1), slice(0, 1), 3),
                                    (slice(G + 1, BW), slice(0, 1), 4)):
                    last = nc.vector.tensor_scalar(base_sb[:, cols], first_ps[:, of], sel[:, 1:2], sel[:, s:s + 1],
                                                   ALU.mult, ALU.add)
                last.then_inc(base_ready, 1)
                dve.wait_ge(base_ready, 1)
                nc.vector.tensor_copy(base_isb[:], base_sb[:]).then_inc(base_ready, 1)
                dve.wait_ge(w_in, 16 * W_LOADS)
                m2 = MUL * MUL
                nc.vector.tensor_scalar(w3_sb[:, 0:m2], w3_raw[:, m2:2 * m2], 1.0 / sqrt(3.0), None, ALU.mult)
                nc.vector.tensor_copy(w3_sb[:, m2:2 * m2], w3_raw[:, 0:m2])
                nc.vector.tensor_copy(w3_sb[:, 2 * m2:WN], w3_raw[:, 2 * m2:WN])

        L0_LOADS = 6
        AHEAD = CH + 1
        l0_in = [sem("l0_in0"), sem("l0_in1")]
        rows_ready, rows_read = sem("rows_ready"), sem("rows_read")
        mlp_ready, silu_done = sem("mlp_ready"), sem("silu_done")
        pick_ready, picked, msg_ready, merged = sem("pick_ready"), sem("picked"), sem("msg_ready"), sem("merged")
        sums_ready, where_ready = sem("sums_ready"), sem("where_ready")
        stored = [sem("stored0"), sem("stored1")]
        msg_made, part_made, left_made, link0 = sem("msg_made"), sem("part_made"), sem("left_made"), sem("link0")
        ADDS = 2 * TILES // NTAB
        landed = sem("landed")
        LANDED_AHEAD = 2 * TILES - CT - NTAB + 1

        lay0 = ExitStack()
        with lay0:
            digit_sb = sb(lay0, "digit_sb", [2, 2, 2, GE], bf16)
            rad_sb = sb(lay0, "rad_sb", [2 * MUL, 2, HALF])
            win_sb = sb(lay0, "win_sb", [P, 2, PARTS, FW], bf16)
            src_i = sb(lay0, "src_i", [P, 2, TILES], i32)
            w_sb = sb(lay0, "w_sb", [P, 2, TILES])
            base_in = sb(lay0, "base_in", [P, 2])
            node_col = sb(lay0, "node_col", [P, 1])
            src_f = sb(lay0, "src_f", [P, TILES])
            to_spare = sb(lay0, "to_spare", [P, TILES])
            pick = sb(lay0, "pick", [P, 2, CT, P], bf16)
            same = sb(lay0, "same", [P, 2, CT, P], bf16)
            later = sb(lay0, "later", [P, CT])
            hop = sb(lay0, "hop", [P, CT])
            where = sb(lay0, "where", [P, 2, TILES], i32)
            msg = sb(lay0, "msg", [P, CT, FW])
            left = sb(lay0, "left", [P, CT, FW])
            msg_b = sb(lay0, "msg_b", [P, 2, PARTS, CT, FW], bf16)
            sums = sb(lay0, "sums", [P, 2, TILES, FW])
            hid1 = sb(lay0, "hid1", [P, 2, 512])
            hid2 = sb(lay0, "hid2", [P, 2, HALF])
            rows_ps = pb(lay0, "rows_ps", [P, 2, 2, 512])
            mlp_ps = pb(lay0, "mlp_ps", [P, 2, 512])
            pick_ps = pb(lay0, "pick_ps", [P, 512])
            sums_ps = pb(lay0, "sums_ps", [P, 512])

            picks, totals = (tile[:, 0:CT * FW].rearrange("p (t f) -> p t f", f=FW) for tile in (pick_ps, sums_ps))

            block = lay0.enter_context(nc.Block("layer0"))

            @block.sync
            def _(sp):
                R = sp.value_load(rounds[0:1, 0:1], min_val=1, max_val=RM)
                with sp.Fori(0, R) as r, sp.Fori(0, G2) as g2:
                    i = r * G2 + g2
                    for s in range(2):
                        g = g2 * 2 + s
                        sp.wait_ge(msg_ready, (i * 2 + s - 1) * CH + AHEAD)
                        sp.wait_ge(merged, (i * 2 + s - 1) * CH + AHEAD)
                        sp.sem_inc(passed, 1)
                        sp.dma_start(digit_sb[:, s, :, :], digits[:, :, bass.ds(g * GE, GE)]).then_inc(l0_in[s], 16)
                        sp.dma_start(rad_sb[:, s, :], radial[bass.ds(g, 1), :, :].rearrange("a p c -> (a p) c")).then_inc(l0_in[s], 16)
                        sp.dma_start(src_i[:, s, :], src_col[:, bass.ds(g * TILES, TILES)]).then_inc(l0_in[s], 16)
                        sp.dma_start(w_sb[:, s, :], w_col[:, bass.ds(g * TILES, TILES)]).then_inc(l0_in[s], 16)
                        at = r * BW + g + 1
                        sp.dma_start(base_in[:, s:s + 1], base_f[:, bass.ds(at, 1)].to_broadcast([P, 1]),
                                     allow_slow_non_contiguous=True).then_inc(l0_in[s], 16)
                        base = sp.value_load(base_i[:, bass.ds(at, 1)], min_val=0, max_val=NT - P)
                        sp.dma_start(win_sb[:, s, :, :].rearrange("p k f -> p (k f)"), h1_tab[bass.ds(base, P), :]).then_inc(l0_in[s], 16)

            @block.tensor
            def _(pe):
                pe.sem_inc(merged, AHEAD)
                R = pe.value_load(rounds[0:1, 0:1], min_val=1, max_val=RM)

                def sum_same(i, c):
                    pe.wait_ge(msg_ready, i * BC + c + 1 + AHEAD)
                    pe.wait_ge(sums_ready, i * BC + c + 2)
                    for t in range(CT):
                        for k in range(PARTS):
                            last = nc.tensor.matmul(totals[:, t, :], same[:, c % 2, t, :], msg_b[:, c % 2, k, t, :],
                                                    start=(k == 0), stop=(k == PARTS - 1))
                    last.then_inc(merged, 1)

                with pe.Fori(0, R) as r, pe.Fori(0, G2) as g2:
                    i = r * G2 + g2
                    for c in range(BC):
                        s, q = divmod(c, CH)
                        if q == 0:
                            pe.wait_ge(l0_in[s], (i + 1) * (16 * L0_LOADS))
                        pe.wait_ge(rows_read, i * BC + c + 1)
                        for a in range(2):
                            last = nc.tensor.matmul(rows_ps[:, c % 2, a, :], place_val[:],
                                                    digit_sb[:, s, a, q * CT * P:(q + 1) * CT * P], start=True, stop=True)
                        last.then_inc(rows_ready, 1)
                        h = q % 2
                        pe.wait_ge(silu_done, i * BC + c + 1)
                        if q < 2:
                            last = nc.tensor.matmul(mlp_ps[:, h, :], w1_bd[:], rad_sb[:, s, h * 512:(h + 1) * 512],
                                                    start=True, stop=True)
                        else:
                            last = nc.tensor.matmul(mlp_ps[:, h, :], w2_bd[:], hid1[:, h, :], start=True, stop=True)
                        last.then_inc(mlp_ready, 1)
                        if c:
                            sum_same(i, c - 1)
                        pe.wait_ge(pick_ready, i * BC + c + 1)
                        for t in range(CT):
                            for k in range(PARTS):
                                last = nc.tensor.matmul(picks[:, t, :], pick[:, c % 2, t, :], win_sb[:, s, k, :],
                                                        start=(k == 0), stop=(k == PARTS - 1))
                        last.then_inc(picked, 1)
                    sum_same(i, BC - 1)

            @block.scalar
            def _(act):
                act.sem_inc(silu_done, 2)
                act.sem_inc(sums_ready, 2)
                for s in range(2):
                    act.dma_start(hidden[G, :, s:s + 1], b1_col[:], allow_slow_non_contiguous=True).then_inc(stored[s], 16)
                R = act.value_load(rounds[0:1, 0:1], min_val=1, max_val=RM)

                def copy_sums(i, c):
                    s, q = divmod(c, CH)
                    act.wait_ge(merged, i * BC + c + 1 + AHEAD)
                    act.wait_ge(landed, i * (2 * TILES) + c * CT + 1)
                    nc.scalar.activation(sums[:, s, q * CT:(q + 1) * CT, :], totals,
                                         ACT.Copy).then_inc(sums_ready, 1)

                with act.Fori(0, R) as r, act.Fori(0, G2) as g2:
                    i = r * G2 + g2
                    for c in range(BC):
                        s, q = divmod(c, CH)
                        h = q % 2
                        act.wait_ge(mlp_ready, i * BC + c + 1)
                        if q < 2:
                            nc.scalar.activation(hid1[:, h, :], mlp_ps[:, h, :], ACT.Silu, bias=b1_col[:]).then_inc(silu_done, 1)
                        else:
                            if q == 2:
                                act.wait_ge(stored[s], i * 16 + 16)
                            nc.scalar.activation(hid2[:, s, h * 512:(h + 1) * 512], mlp_ps[:, h, :], ACT.Silu,
                                                 bias=b2_col[:]).then_inc(silu_done, 1)
                        if q == 3:
                            act.wait_ge(silu_done, i * BC + c + 1 + 2)
                            act.dma_start(hidden[bass.ds(g2 * 2 + s, 1), :, :].rearrange("a p c -> (a p) c"),
                                          hid2[:, s, :]).then_inc(stored[s], 16)
                        if c:
                            copy_sums(i, c - 1)
                        act.wait_ge(msg_made, i * BC + c + 1)
                        nc.scalar.activation(msg_b[:, c % 2, 0], msg[:], ACT.Copy).then_inc(part_made, 1)
                        act.wait_ge(left_made, i * BC + c + 1)
                        nc.scalar.activation(msg_b[:, c % 2, 1], left[:], ACT.Copy).then_inc(part_made, 1)
                    copy_sums(i, BC - 1)
                for s in range(2):
                    act.wait_ge(stored[s], R * (G2 * 16) + 16)
                    act.sem_inc(passed, 1)

            @block.vector
            def _(dve):
                dve.sem_inc(msg_ready, AHEAD)
                dve.sem_inc(rows_read, 2)
                R = dve.value_load(rounds[0:1, 0:1], min_val=1, max_val=RM)
                LINKS = 2 * (2 + CH)
                with dve.Fori(0, R) as r, dve.Fori(0, G2) as g2:
                    i = r * G2 + g2
                    link = 0
                    for c in range(BC):
                        s, q = divmod(c, CH)
                        dve.wait_ge(msg_ready, i * BC + c + AHEAD)
                        if q == 0:
                            dve.wait_ge(l0_in[s], (i + 1) * (16 * L0_LOADS))
                            nc.vector.tensor_tensor(node_col[:], iota_col[:], base_in[:, s:s + 1], ALU.add)
                            nc.vector.tensor_copy(src_f[:], src_i[:, s, :]).then_inc(link0, 1)
                            link += 1
                            dve.wait_ge(link0, i * LINKS + link)
                            nc.vector.tensor_scalar(to_spare[:], src_f[:], -1.0, spare_col[:], ALU.mult, ALU.add).then_inc(link0, 1)
                            link += 1
                            dve.wait_ge(link0, i * LINKS + link)
                        dve.wait_ge(rows_ready, i * BC + c + 1)
                        nc.vector.tensor_scalar(pick[:, c % 2, :, :].rearrange("p t e -> p (t e)"), rows_ps[:, c % 2, 0, :],
                                                node_col[:], None, ALU.is_equal).then_inc(pick_ready, 1)
                        dve.wait_ge(merged, i * BC + c - 1 + AHEAD)

                        def same_src(t):
                            return nc.vector.scalar_tensor_tensor(
                                same[:, c % 2, t, :], rows_ps[:, c % 2, 1, t * P:(t + 1) * P],
                                src_f[:, q * CT + t:q * CT + t + 1], upper[:], ALU.is_equal, ALU.mult,
                                accum_out=later[:, t:t + 1])

                        same_src(0)
                        same_src(1)
                        m = msg_b[:, c % 2]
                        dve.wait_ge(picked, i * BC + c + 1)
                        nc.vector.tensor_tensor(msg[:], picks, w_sb[:, s, q * CT:(q + 1) * CT].unsqueeze(2).to_broadcast([P, CT, FW]),
                                                ALU.mult).then_inc(msg_made, 1)
                        same_src(2)
                        dve.wait_ge(part_made, i * (2 * BC) + 2 * c + 1)
                        nc.vector.tensor_tensor(left[:], msg[:], m[:, 0], ALU.subtract).then_inc(left_made, 1)
                        same_src(3).then_inc(rows_read, 1)
                        dve.wait_ge(rows_read, i * BC + c + 1 + 2)
                        nc.vector.scalar_tensor_tensor(hop[:], later[:], 1.5, to_spare[:, q * CT:(q + 1) * CT],
                                                       ALU.is_gt, ALU.mult).then_inc(link0, 1)
                        link += 1
                        dve.wait_ge(link0, i * LINKS + link)
                        dve.wait_ge(landed, i * (2 * TILES) + c * CT + 1)
                        nc.vector.tensor_tensor(where[:, s, q * CT:(q + 1) * CT], src_f[:, q * CT:(q + 1) * CT], hop[:],
                                                ALU.add).then_inc(where_ready, 1)
                        dve.wait_ge(part_made, i * (2 * BC) + 2 * c + 2)
                        nc.vector.tensor_tensor(m[:, 2], left[:], m[:, 1], ALU.subtract).then_inc(msg_ready, 1)

            @block.gpsimd
            def _(pool):
                pool.sem_inc(landed, LANDED_AHEAD)
                R = pool.value_load(rounds[0:1, 0:1], min_val=1, max_val=RM)
                pool.wait_ge(l0_in[0], 16 * L0_LOADS)
                for k in range(EARLY, NTAB):
                    clear_table(pool, k)
                with pool.Fori(0, R) as r, pool.Fori(0, G2) as g2:
                    i = r * G2 + g2
                    for t in range(2 * TILES):
                        c = t // CT
                        if t % CT == 0:
                            pool.wait_ge(where_ready, i * BC + c + 1)
                            pool.wait_ge(sums_ready, i * BC + c + 1 + 2)
                        pool.wait_ge(added[t % NTAB], i * (16 * ADDS) + 16 * (t // NTAB) + 16)
                        pool.sem_inc(landed, 1)
                        s, u = divmod(t, TILES)
                        pool.indirect_dma_start(
                            lap_tab[t % NTAB], bass.IndirectOffsetOnAxis(ap=where[:, s, u:u + 1], axis=0),
                            sums[:, s, u, :], None, compute_op=ALU.add).then_inc(added[t % NTAB], 16)
                for k in range(NTAB):
                    pool.wait_ge(added[k], R * (G2 * 16 * ADDS) + 16)
                    pool.sem_inc(passed, 1)

        win_out = sem("win_out")
        laps_in = [[sem(f"laps_in{h}_{k}") for k in range(NTAB)] for h in range(2)]
        self_t, self_c, self_ready, agg_ready = sem("self_t"), sem("self_c"), sem("self_ready"), sem("agg_ready")
        centered2, squared2, var_ready2, std_ready2, h2_ready, nodes_out = (
            sem("centered2"), sem("squared2"), sem("var_ready2"), sem("std_ready2"), sem("h2_ready"), sem("nodes_out"))

        L1_LOADS = 5
        DONE = BC
        l1_in = [sem("l1_in0"), sem("l1_in1")]
        got = [sem(f"got{c}") for c in range(BC)]
        delta_ready, onehot_ready, scaled_ready = sem("delta_ready"), sem("onehot_ready"), sem("scaled_ready")
        paths_ready, parts_ready, agg_done, acc_read = sem("paths_ready"), sem("parts_ready"), sem("agg_done"), sem("acc_read")
        win_in, win_ready = sem("win_in"), sem("win_ready")
        link1, sq_step = sem("link1"), sem("sq_step")
        ones_ready = sem("ones_ready")

        lay1 = ExitStack()
        with lay1:
            hid_sb = sb(lay1, "hid_sb", [HR + 1, 2, GE])
            idx_sb = sb(lay1, "idx_sb", [P, 2, TILES], i32)
            dst_sb = sb(lay1, "dst_sb", [P, 2, TILES], i32)
            sh_sb = sb(lay1, "sh_sb", [P, 2, TILES, 4])
            base_sb1 = sb(lay1, "base_sb1", [P, 2])
            delta = sb(lay1, "delta", [P, 2, TILES])
            hs = sb(lay1, "hs", [P, 2, TILES, F])
            dist = sb(lay1, "dist", [P, CT, P])
            onehot = sb(lay1, "onehot", [P, 2, CT, P])
            scaled = sb(lay1, "scaled", [P, 2, CT, F + MUL])
            vsh = sb(lay1, "vsh", [P, CT, MUL, 3])
            prod01 = sb(lay1, "prod01", [P, CT, MUL, MUL])
            prod10 = sb(lay1, "prod10", [P, CT, 3, MUL * MUL])
            vec0 = sb(lay1, "vec0", [P, CT, MUL])
            parts = sb(lay1, "parts", [P, 2, CT, RC])
            red = sb(lay1, "red", [P, F])
            win_old = sb(lay1, "win_old", [P, F])
            win_new = sb(lay1, "win_new", [P, F])
            paths_ps = pb(lay1, "paths_ps", [P, 2, CT, WN])
            acc_ps = pb(lay1, "acc_ps", [P, 2, 512])
            m2 = MUL * MUL
            laps = [sb(lay1, f"laps{k}", [NP, C, FW]) for k in range(NTAB)]
            mean = sb(lay1, "mean2", [NP, C])
            std = sb(lay1, "std2", [NP, C])
            h2_sb = sb(lay1, "h2_sb", [NP, C * F])
            h2_t = sb(lay1, "h2_t", [P, 2, 4, NP])
            t_ps, self_ps = (paths_ps[:, k].rearrange("p t n -> p (t n)").rearrange("p (b n) -> p b n", b=2) for k in range(2))
            halves = (slice(0, C // 2), slice(C // 2, C))
            xc = [laps[1][:, n, 0:F] for n in halves]
            sq = [laps[2][:, n, 0:F] for n in halves]
            quads = C * F // P
            batches = [range(k, min(k + 4, quads)) for k in range(0, quads, 4)]

            block = lay1.enter_context(nc.Block("layer1"))

            @block.sync
            def _(sp):
                for h, n in enumerate(halves):
                    cols = slice(n.start * FW, n.stop * FW)
                    for k in range(NTAB):
                        sp.dma_start(laps[k][:].rearrange("p c f -> p (c f)")[:, cols],
                                     lap_tab[k][0:N, :].rearrange("(p c) f -> p (c f)", p=NP)[:, cols]).then_inc(laps_in[h][k], 16)
                sp.dma_start(hidden[G], hidden[0]).then_inc(nodes_out, 16)
                for h, n in enumerate(halves):
                    cols = slice(n.start * F, n.stop * F)
                    sp.wait_ge(h2_ready, h + 1)
                    sp.dma_start(h2_tab[0:N, :].rearrange("(p c) f -> p (c f)", p=NP)[:, cols], h2_sb[:, cols]).then_inc(nodes_out, 16)
                sp.wait_ge(nodes_out, 48)
                R = sp.value_load(rounds[0:1, 0:1], min_val=1, max_val=RM)

                def load(s, r, g):
                    for h in range(2):
                        sp.dma_start(hid_sb[0:HR, s, h * HALF:(h + 1) * HALF],
                                     hidden[bass.ds(g, 1), h * HR:(h + 1) * HR, :].rearrange("a p c -> (a p) c")).then_inc(l1_in[s], 16)
                    sp.dma_start(idx_sb[:, s, :], src_col[:, bass.ds(g * TILES, TILES)]).then_inc(l1_in[s], 16)
                    sp.dma_start(dst_sb[:, s, :], dst_col[:, bass.ds(g * TILES, TILES)]).then_inc(l1_in[s], 16)
                    sp.dma_start(sh_sb[:, s, :, :].rearrange("p t c -> p (t c)"),
                                 sh_col[:, bass.ds(g * (TILES * 4), TILES * 4)]).then_inc(l1_in[s], 16)
                    sp.dma_start(base_sb1[:, s:s + 1], base_f[:, bass.ds(r * BW + g + 1, 1)].to_broadcast([P, 1]),
                                 allow_slow_non_contiguous=True).then_inc(l1_in[s], 16)

                def add_window(n, at):
                    sp.wait_ge(win_out, n * 16 + 16)
                    sp.sem_inc(passed, 1)
                    base = sp.value_load(base_i[:, bass.ds(at, 1)], min_val=0, max_val=NT - P)
                    sp.dma_start(win_old[:], agg_tab[bass.ds(base, P), :]).then_inc(win_in, 16)
                    sp.wait_ge(win_ready, n + 1)
                    sp.dma_start(agg_tab[bass.ds(base, P), :], win_new[:]).then_inc(win_out, 16)

                zero = sp.snap(R * 0)
                load(0, zero, zero)
                with sp.Fori(0, R) as r, sp.Fori(0, G2) as g2:
                    i = r * G2 + g2
                    for s in range(2):
                        n, g = i * 2 + s, g2 * 2 + s
                        sp.wait_ge(parts_ready, n * CH + DONE)
                        load(1 - s, r, g + 1)
                        add_window(n, r * BW + g)
                add_window(R * G, (R - 1) * BW + G)
                sp.wait_ge(win_out, (R * G + 2) * 16)
                sp.wait_ge(l1_in[0], (R * G2 + 1) * (16 * (L1_LOADS + 1)))
                sp.sem_inc(passed, 1)

            @block.gpsimd
            def _(pool):
                pool.wait_ge(nodes_out, 48)
                R = pool.value_load(rounds[0:1, 0:1], min_val=1, max_val=RM)
                with pool.Fori(0, R) as r, pool.Fori(0, G2) as g2:
                    i = r * G2 + g2
                    for c in range(BC):
                        s, q = divmod(c, CH)
                        if q == 0:
                            pool.wait_ge(l1_in[s], (i + 1) * (16 * (L1_LOADS + 1)))
                        pool.wait_ge(parts_ready, i * BC + c + 1)
                        pool.sem_inc(passed, 1)
                        for t in range(q * CT, (q + 1) * CT):
                            pool.indirect_dma_start(hs[:, s, t, :], None, h2_tab,
                                                    bass.IndirectOffsetOnAxis(ap=idx_sb[:, s, t:t + 1], axis=0)).then_inc(got[c], 16)

            @block.scalar
            def _(act):
                for h, n in enumerate(halves):
                    act.wait_ge(centered2, h + 1)
                    nc.scalar.activation(sq[h], xc[h], ACT.Square).then_inc(squared2, 1)
                    act.wait_ge(var_ready2, h + 1)
                    nc.scalar.activation(std[:, n], mean[:, n], ACT.Sqrt, scale=1.0 / F, bias=eps_col[0:NP, :]).then_inc(std_ready2, 1)
                for b, quad in enumerate(batches):
                    act.wait_ge(self_t, b + 1)
                    if b >= 2:
                        act.wait_ge(self_ready, b - 1)
                    nc.scalar.activation(h2_t[:, b % 2, 0:len(quad), :],
                                         t_ps[:, b % 2, 0:len(quad) * NP].rearrange("p (q n) -> p q n", n=NP),
                                         ACT.Copy).then_inc(self_c, 1)
                act.wait_ge(agg_ready, len(batches))
                act.dma_start(agg_tab[0:N, :].rearrange("(p c) f -> p (c f)", p=NP),
                              x_sb[:].rearrange("p c f -> p (c f)")).then_inc(win_out, 16)
                act.sem_inc(onehot_ready, 1)
                R = act.value_load(rounds[0:1, 0:1], min_val=1, max_val=RM)
                with act.Fori(0, R) as r, act.Fori(0, G2) as g2:
                    i = r * G2 + g2
                    for c in range(BC):
                        s, q = divmod(c, CH)
                        act.wait_ge(got[c], (i + 1) * (16 * CT))
                        act.wait_ge(parts_ready, i * BC + c - 1 + DONE)
                        for t in range(CT):
                            last = nc.scalar.activation(scaled[:, c % 2, t, MUL:MUL + F], hs[:, s, q * CT + t, :], ACT.Copy,
                                                        scale=sh_sb[:, s, q * CT + t, 0:1])
                        last.then_inc(scaled_ready, 1)
                        act.wait_ge(onehot_ready, i * BC + c + 1)
                        act.wait_ge(delta_ready, i * 2 + s + 1)
                        for t in range(CT):
                            last = nc.scalar.activation(dist[:, t, :], iota_row[:], ACT.Square,
                                                        bias=delta[:, s, q * CT + t:q * CT + t + 1])
                        last.then_inc(sq_step, 1)
                        act.wait_ge(sq_step, i * BC + c + 1)
                        act.wait_ge(agg_done, i * BC + c + 1)
                        nc.scalar.activation(onehot[:, c % 2, :, :].rearrange("p t e -> p (t e)"),
                                             dist[:].rearrange("p t e -> p (t e)"),
                                             ACT.Relu, scale=-2.0, bias=1.0).then_inc(onehot_ready, 1)

            @block.tensor
            def _(pe):
                pe.wait_ge(h2_ready, 2)
                for b, quad in enumerate(batches):
                    if b >= 2:
                        pe.wait_ge(self_c, b - 1)
                    for k, q in enumerate(quad):
                        last = nc.tensor.transpose(t_ps[:, b % 2, k * NP:(k + 1) * NP], h2_sb[:, q * P:(q + 1) * P],
                                                   ident[0:NP, 0:NP])
                    last.then_inc(self_t, 1)
                    pe.wait_ge(self_c, b + 1)
                    if b >= 2:
                        pe.wait_ge(agg_ready, b - 1)
                    for k, q in enumerate(quad):
                        last = nc.tensor.matmul(self_ps[0:NP, b % 2, k * P:(k + 1) * P], h2_t[:, b % 2, k, :], self_bd[:],
                                                start=True, stop=True)
                    last.then_inc(self_ready, 1)
                pe.wait_ge(agg_ready, len(batches))
                pe.sem_inc(agg_done, 2)
                R = pe.value_load(rounds[0:1, 0:1], min_val=1, max_val=RM)
                pe.wait_ge(ones_ready, 1)

                def path_weights(i, c):
                    s, q = divmod(c % BC, CH)
                    if q == 0:
                        pe.wait_ge(l1_in[s], (i + c // BC + 1) * (16 * (L1_LOADS + 1)))
                    pe.wait_ge(parts_ready, i * BC + c - 1 + DONE)
                    for t in range(CT):
                        e = (q * CT + t) * P
                        last = nc.tensor.matmul(paths_ps[:, c % 2, t, :], hid_sb[:, s, e:e + P], w3_sb[:], start=True, stop=True)
                    last.then_inc(paths_ready, 1)

                def aggregate(i, c):
                    s, q = divmod(c, CH)
                    pe.wait_ge(onehot_ready, i * BC + c + 2)
                    pe.wait_ge(parts_ready, i * BC + c + 1 + DONE)
                    if q == 0:
                        pe.wait_ge(acc_read, i * 2 + s + 1)
                    for t in range(CT):
                        last = nc.tensor.matmul(acc_ps[:, s, 0:RC], onehot[:, c % 2, t, :], parts[:, c % 2, t, :],
                                                start=(q == 0 and t == 0), stop=(q == CH - 1 and t == CT - 1))
                    last.then_inc(agg_done, 1)

                path_weights(0, 0)
                with pe.Fori(0, R) as r, pe.Fori(0, G2) as g2:
                    i = r * G2 + g2
                    for c in range(BC):
                        path_weights(i, c + 1)
                        if c:
                            aggregate(i, c - 1)
                    aggregate(i, BC - 1)

            @block.vector
            def _(dve):
                dve.sem_inc(parts_ready, DONE)
                dve.sem_inc(acc_read, 1)
                nc.vector.memset(hid_sb[HR:HR + 1, :, :], 1.0).then_inc(ones_ready, 1)
                nc.vector.memset(acc_ps[:, 1, 0:RC], 0.0)

                def sum_laps(h, tabs):
                    for k in tabs:
                        dve.wait_ge(laps_in[h][k], 16)
                        if k:
                            then(dve, nc.vector.tensor_tensor(laps[0][:, halves[h], :], laps[0][:, halves[h], :],
                                                              laps[k][:, halves[h], :], ALU.add))

                def new_x(h):
                    n = halves[h]
                    lap, own = laps[0][:, n, 0:F], laps[1][:, n, 0:F]
                    then(dve, nc.vector.tensor_tensor(own, h1_sb[:, n, 0:F], laps[0][:, n, F:FW].to_broadcast([NP, C // 2, F]), ALU.mult))
                    then(dve, nc.vector.tensor_tensor(lap, lap, own, ALU.subtract))
                    then(dve, nc.vector.tensor_tensor(x_sb[:, n, :], x_sb[:, n, :], lap, ALU.add))
                    center(dve, x_sb[:, n, :], mean[:, n], xc[h], centered2)

                def variance(h):
                    dve.wait_ge(squared2, h + 1)
                    nc.vector.tensor_reduce(mean[:, halves[h]], sq[h], axis=AX, op=ALU.add).then_inc(var_ready2, 1)

                def new_h(h):
                    dve.wait_ge(std_ready2, h + 1)
                    normalise(dve, std[:, halves[h]], xc[h], h2_sb[:].rearrange("p (c f) -> p c f", f=F)[:, halves[h], :], h2_ready)

                sum_laps(0, range(NTAB))
                new_x(0)
                sum_laps(1, range(3))
                variance(0)
                sum_laps(1, range(3, 5))
                new_h(0)
                sum_laps(1, range(5, NTAB))
                new_x(1)
                variance(1)
                new_h(1)
                flat = x_sb[:].rearrange("p c f -> p (c f)")
                for b, quad in enumerate(batches):
                    dve.wait_ge(self_ready, b + 1)
                    cols = flat[:, quad[0] * P:(quad[-1] + 1) * P]
                    nc.vector.scalar_tensor_tensor(cols, self_ps[0:NP, b % 2, 0:len(quad) * P], SELF_SCALE, cols,
                                                   ALU.mult, ALU.add).then_inc(agg_ready, 1)
                R = dve.value_load(rounds[0:1, 0:1], min_val=1, max_val=RM)

                def add_window(n, s):
                    dve.wait_ge(agg_done, n * CH + 2)
                    nc.vector.tensor_reduce(red[:, 0:MUL], acc_ps[:, s, 0:RS].rearrange("p (u w) -> p w u", w=MUL), axis=AX, op=ALU.add)
                    nc.vector.tensor_reduce(red[:, MUL:F], acc_ps[:, s, RS:RC].rearrange("p (i u w) -> p i w u", i=3, w=MUL),
                                            axis=AX, op=ALU.add).then_inc(acc_read, 1)
                    dve.wait_ge(acc_read, n + 2)
                    dve.wait_ge(win_in, (n + 1) * 16)
                    nc.vector.scalar_tensor_tensor(win_new[:, 0:MUL], red[:, 0:MUL], MSG_SCALE, win_old[:, 0:MUL], ALU.mult, ALU.add)
                    nc.vector.scalar_tensor_tensor(win_new[:, MUL:F].rearrange("p (w i) -> p w i", i=3),
                                                   red[:, MUL:F].rearrange("p (i w) -> p w i", i=3), MSG_SCALE,
                                                   win_old[:, MUL:F].rearrange("p (w i) -> p w i", i=3),
                                                   ALU.mult, ALU.add).then_inc(win_ready, 1)

                with dve.Fori(0, R) as r, dve.Fori(0, G2) as g2:
                    i = r * G2 + g2
                    for c in range(BC):
                        s, q = divmod(c, CH)
                        if q == 0:
                            dve.wait_ge(l1_in[s], (i + 1) * (16 * (L1_LOADS + 1)))
                            nc.vector.tensor_scalar(delta[:, s, :], dst_sb[:, s, :], -1.0, base_sb1[:, s:s + 1],
                                                    ALU.mult, ALU.add).then_inc(delta_ready, 1)
                        tiles = slice(q * CT, (q + 1) * CT)
                        sc, W, out_c = scaled[:, c % 2], paths_ps[:, c % 2], parts[:, c % 2]
                        dve.wait_ge(got[c], (i + 1) * (16 * CT))
                        nc.vector.tensor_tensor(vsh[:], hs[:, s, tiles, MUL:F].rearrange("p t (u i) -> p t u i", i=3),
                                                sh_sb[:, s, tiles, 1:4].unsqueeze(2).to_broadcast([P, CT, MUL, 3]),
                                                ALU.mult).then_inc(link1, 1)
                        dve.wait_ge(paths_ready, i * BC + c + 1)
                        nc.vector.tensor_tensor(prod01[:], W[:, :, 2 * m2:3 * m2].rearrange("p t (u w) -> p t u w", w=MUL),
                                                hs[:, s, tiles, 0:MUL].unsqueeze(3).to_broadcast([P, CT, MUL, MUL]), ALU.mult)
                        dve.wait_ge(link1, i * (3 * BC) + 3 * c + 1)
                        nc.vector.tensor_reduce(sc[:, :, 0:MUL], vsh[:], axis=AX, op=ALU.add).then_inc(link1, 1)
                        dve.wait_ge(scaled_ready, i * BC + c + 1)
                        dve.wait_ge(parts_ready, i * BC + c + DONE)
                        for k in range(3):
                            nc.vector.tensor_tensor(
                                prod10[:, :, k, :].rearrange("p t (u w) -> p t u w", w=MUL),
                                W[:, :, 3 * m2:4 * m2].rearrange("p t (u w) -> p t u w", w=MUL),
                                sc[:, :, 2 * MUL + k:2 * MUL + F - MUL:3].unsqueeze(3).to_broadcast([P, CT, MUL, MUL]), ALU.mult)
                        dve.wait_ge(link1, i * (3 * BC) + 3 * c + 2)
                        nc.vector.tensor_reduce(vec0[:], prod01[:].rearrange("p t u w -> p t w u"), axis=AX,
                                                op=ALU.add).then_inc(link1, 1)
                        dve.wait_ge(agg_done, i * BC + c + 1)
                        nc.vector.tensor_tensor(out_c[:, :, 0:RS].rearrange("p t (k w) -> p t k w", w=MUL),
                                                W[:, :, 0:2 * m2].rearrange("p t (k w) -> p t k w", w=MUL),
                                                sc[:, :, 0:2 * MUL].unsqueeze(3).to_broadcast([P, CT, 2 * MUL, MUL]), ALU.mult)
                        dve.wait_ge(link1, i * (3 * BC) + 3 * c + 3)
                        vec = out_c[:, :, RS:RC].rearrange("p t (i k) -> p t i k", i=3)
                        nc.vector.tensor_tensor(vec[:, :, :, 0:m2 // 2], prod10[:, :, :, 0:m2 // 2], prod10[:, :, :, m2 // 2:m2], ALU.add)
                        nc.vector.tensor_tensor(vec[:, :, :, m2 // 2:SUMS * MUL], vec0[:].unsqueeze(2).to_broadcast([P, CT, 3, MUL]),
                                                sh_sb[:, s, tiles, 1:4].unsqueeze(3).to_broadcast([P, CT, 3, MUL]),
                                                ALU.mult).then_inc(parts_ready, 1)
                        if q == 2:
                            add_window(i * 2 + s, 1 - s)
                add_window(R * G, 1)

        result_out = sem("result_out")
        with ExitStack() as fin:
            block = fin.enter_context(nc.Block("result"))

            @block.sync
            def _(sp):
                sp.dma_start(out.rearrange("(p c) f -> p (c f)", p=P - 3),
                             agg_tab[0:N, :].rearrange("(p c) f -> p (c f)", p=P - 3)).then_inc(result_out, 16)
                sp.wait_ge(result_out, 16)


def laid_out(x, src, dst, edge_attr_4, edge_attr_8, edge_weight, weights):
    import numpy as np
    n, e = x.shape[0], src.shape[0]
    groups = -(-e // GE)
    groups += groups % 2
    pad = groups * GE - e

    def padded(a, v):
        return np.concatenate([a, np.full((pad,) + a.shape[1:], v, a.dtype)])

    def columns(a):
        a = a.reshape(groups * TILES, P, -1).transpose(1, 0, 2)
        a = np.concatenate([a, a[:, :TILES]], axis=1)
        return np.ascontiguousarray(a.reshape(P, -1))

    src, dst = (padded(a.astype(np.int32), n) for a in (src, dst))
    sh, rad, w = padded(edge_attr_4, 0), padded(edge_attr_8, 0), padded(edge_weight, 0)
    rad = np.ascontiguousarray(rad.reshape(groups, 2, HALF, MUL).transpose(0, 1, 3, 2).reshape(groups, 2 * MUL, HALF))
    return dict(x=x, src_row=src, dst_row=dst, src_col=columns(src), dst_col=columns(dst), w_col=columns(w),
                sh_col=columns(sh), radial=rad, **weights)


def kernel(**inputs):
    import numpy as _np
    import concourse.bacc as _bacc
    from concourse import mybir as _mybir
    from concourse.bass_utils import run_bass_kernel_spmd as _run

    a = {k: _np.asarray(v) for k, v in inputs.items()}
    weights = {k: a["L1_gnn_" + k] for k in ("W1", "b1", "W2", "b2", "W3", "b3", "Ws", "Wv")}
    arrays = laid_out(a["x"], a["src"], a["dst"], a["edge_attr_4"], a["edge_attr_8"], a["edge_weight"], weights)
    nc = _bacc.Bacc("TRN2", target_bir_lowering=False, num_devices=1)
    args = {k: nc.dram_tensor(f"in_{k}_dram", v.shape, _mybir.dt.from_np(v.dtype), kind="ExternalInput").ap()
            for k, v in arrays.items()}
    out = nc.dram_tensor("out_dram", a["x"].shape, _mybir.dt.float32, kind="ExternalOutput").ap()
    gnn_program(nc, **args, out=out)
    r = _run(nc, [{f"in_{k}_dram": _np.ascontiguousarray(v) for k, v in arrays.items()}], core_ids=[0])
    return r.results[0]["out_dram"]
```
